# Optimizing a Trainium2 kernel written in Bass

```python
import numpy as np
import jax
import jax.numpy as jnp

def _softmax(x, axis=-1):
    return jax.nn.softmax(x, axis=axis)

def _gelu(x):
    return jax.nn.gelu(x, approximate=True)

def _silu(x):
    return jax.nn.silu(x)

def _sigmoid(x):
    return jax.nn.sigmoid(x)

def _layernorm(x, axis=-1, eps=1e-05):
    m = jnp.mean(x, axis=axis, keepdims=True)
    v = jnp.var(x, axis=axis, keepdims=True)
    return (x - m) / jnp.sqrt(v + eps)

def _scatter_add(tgt, idx, src, axis=0):
    return tgt.at[idx].add(src)

def _segment_sum(src, seg, n):
    return jax.ops.segment_sum(src, seg, n)
kernel_name = 'mk_vit_tower_d1_tok_img2048_r4_2ebb69'

def setup_inputs(seed: int=0):
    np.random.seed(seed)
    _w = jnp.asarray

    def _rec_inputs():
        import jax
        import jax.numpy as jnp
        _rk = jax.random.key(seed)
        x = jax.random.uniform(jax.random.fold_in(_rk, 1), (4, 1, 128, 128), jnp.float32, 0.0, 1)
        return x
    x = _rec_inputs()

    def _L0_tok_setup():
        import jax, jax.numpy as jnp
        import numpy as np
        K = 8
        BLOCK_LEN = K * K
        NBLOCKS = 512

        def _unfold(img):
            B, C, H, W = img.shape
            p = img.reshape(B, C, H // K, K, W // K, K)
            p = p.transpose(0, 1, 3, 5, 2, 4)
            return p.reshape(B, C * K * K, H // K * (W // K))
        key = jax.random.key(seed)
        k1, k2 = jax.random.split(key)
        blocks = jax.random.uniform(k1, (NBLOCKS, BLOCK_LEN), dtype=jnp.float32)
        target_img = jax.random.uniform(k2, (2, 1, 256, 256), dtype=jnp.float32)
        return {'blocks': blocks, 'target_img': target_img}
    _L0_tok_all = _L0_tok_setup()
    _L0_tok_in = {k: v for k, v in _L0_tok_all.items() if k in ('blocks',)}
    del _L0_tok_all

    def _L0_attn_setup():
        import jax, jax.numpy as jnp
        import numpy as np
        EPS = 1e-15
        HEAD_DIM = 32
        PAD_VAL = 1.0
        key = jax.random.key(seed)
        k1, k2, k3, k4 = jax.random.split(key, 4)
        B, N, C = (2, 1024, 512)
        s = 1.0 / np.sqrt(C).astype(np.float32)
        x = jax.random.normal(k1, (B, N, C), jnp.float32)
        w_qkv = jax.random.normal(k2, (3 * C, C), jnp.float32) * s
        w_proj = jax.random.normal(k3, (C, C), jnp.float32) * s
        b_proj = jax.random.normal(k4, (C,), jnp.float32) * 0.01
        return {'x': x, 'w_qkv': w_qkv, 'w_proj': w_proj, 'b_proj': b_proj}
    _L0_attn_all = _L0_attn_setup()
    _L0_attn_in = {k: v for k, v in _L0_attn_all.items() if k in ('w_qkv', 'w_proj', 'b_proj')}
    del _L0_attn_all

    def _L0_ffn_setup():
        import jax, jax.numpy as jnp
        import numpy as np

        @jax.custom_vjp
        def ste_sign(x):
            return jnp.sign(x)

        def _ste_fwd(x):
            return (jnp.sign(x), None)

        def _ste_bwd(_, g):
            return (g,)
        ste_sign.defvjp(_ste_fwd, _ste_bwd)
        D_MODEL = 512
        D_HIDDEN = 2048
        key = jax.random.key(seed)
        k_x, k_up, k_dn = jax.random.split(key, 3)
        x = jax.random.normal(k_x, (2, 512, D_MODEL), dtype=jnp.float32)
        up_weight = jax.random.normal(k_up, (D_HIDDEN, D_MODEL), dtype=jnp.float32) * 0.02
        down_weight = jax.random.normal(k_dn, (D_MODEL, D_HIDDEN), dtype=jnp.float32) * 0.02
        up_scale = jnp.ones((D_HIDDEN,), dtype=jnp.float32)
        down_scale = jnp.ones((D_MODEL,), dtype=jnp.float32)
        output_scale = jnp.ones((1,), dtype=jnp.float32)
        return {'x': x, 'up_weight': up_weight, 'down_weight': down_weight, 'up_scale': up_scale, 'down_scale': down_scale, 'output_scale': output_scale}
    _L0_ffn_all = _L0_ffn_setup()
    _L0_ffn_in = {k: v for k, v in _L0_ffn_all.items() if k in ('up_weight', 'down_weight', 'up_scale', 'down_scale', 'output_scale')}
    del _L0_ffn_all
    return {'x': x, 'L0_tok_blocks': _L0_tok_in['blocks'], 'L0_attn_w_qkv': _L0_attn_in['w_qkv'], 'L0_attn_w_proj': _L0_attn_in['w_proj'], 'L0_attn_b_proj': _L0_attn_in['b_proj'], 'L0_ffn_up_weight': _L0_ffn_in['up_weight'], 'L0_ffn_down_weight': _L0_ffn_in['down_weight'], 'L0_ffn_up_scale': _L0_ffn_in['up_scale'], 'L0_ffn_down_scale': _L0_ffn_in['down_scale'], 'L0_ffn_output_scale': _L0_ffn_in['output_scale']}

def reference(x, L0_tok_blocks, L0_attn_w_qkv, L0_attn_w_proj, L0_attn_b_proj, L0_ffn_up_weight, L0_ffn_down_weight, L0_ffn_up_scale, L0_ffn_down_scale, L0_ffn_output_scale):
    import jax
    import jax.numpy as jnp

    def _L0_tok_ref(blocks, target_img):
        import jax, jax.numpy as jnp
        import numpy as np
        K = 8
        BLOCK_LEN = K * K
        NBLOCKS = 512

        def _unfold(img):
            B, C, H, W = img.shape
            p = img.reshape(B, C, H // K, K, W // K, K)
            p = p.transpose(0, 1, 3, 5, 2, 4)
            return p.reshape(B, C * K * K, H // K * (W // K))
        uf = _unfold(target_img)
        sq_a = jnp.sum(uf * uf, axis=1)
        sq_b = jnp.sum(blocks * blocks, axis=1)
        cross = jnp.einsum('bkl,nk->bln', uf, blocks)
        mse = (sq_a[:, :, None] - 2.0 * cross + sq_b[None, None, :]) / BLOCK_LEN
        return mse

    def _L0_attn_ref(x, w_qkv, w_proj, b_proj):
        import jax, jax.numpy as jnp
        import numpy as np
        EPS = 1e-15
        HEAD_DIM = 32
        PAD_VAL = 1.0
        B, N, C = x.shape
        d = HEAD_DIM
        h = C // d
        qkv = (x @ w_qkv.T).reshape(B, N, 3, C)
        q, k, v = (qkv[:, :, 0], qkv[:, :, 1], qkv[:, :, 2])

        def to_heads(t):
            return t.reshape(B, N, h, d).transpose(0, 2, 3, 1)
        q = jax.nn.relu(to_heads(q))
        k = jax.nn.relu(to_heads(k))
        v = to_heads(v)
        v_pad = jnp.pad(v, ((0, 0), (0, 0), (0, 1), (0, 0)), constant_values=PAD_VAL)
        vk = jnp.einsum('bhen,bhdn->bhed', v_pad, k)
        out = jnp.einsum('bhed,bhdn->bhen', vk, q)
        out = out[:, :, :-1] / (out[:, :, -1:] + EPS)
        out = out.reshape(B, C, N).transpose(0, 2, 1)
        return out @ w_proj.T + b_proj

    def _L0_ffn_ref(x, up_weight, down_weight, up_scale, down_scale, output_scale):
        import jax, jax.numpy as jnp
        import numpy as np

        @jax.custom_vjp
        def ste_sign(x):
            return jnp.sign(x)

        def _ste_fwd(x):
            return (jnp.sign(x), None)

        def _ste_bwd(_, g):
            return (g,)
        ste_sign.defvjp(_ste_fwd, _ste_bwd)
        D_MODEL = 512
        D_HIDDEN = 2048
        up_w = ste_sign(up_weight)
        down_w = ste_sign(down_weight)
        hidden = jnp.einsum('bsd,hd->bsh', x, up_w) * up_scale
        hidden = jax.nn.relu(hidden)
        out = jnp.einsum('bsh,dh->bsd', hidden, down_w) * down_scale
        return out * output_scale
    h = _L0_tok_ref(L0_tok_blocks, x)
    h = h + _L0_attn_ref(_layernorm(h, axis=-1), L0_attn_w_qkv, L0_attn_w_proj, L0_attn_b_proj)
    h = h + _L0_ffn_ref(_layernorm(h, axis=-1), L0_ffn_up_weight, L0_ffn_down_weight, L0_ffn_up_scale, L0_ffn_down_scale, L0_ffn_output_scale)
    return h

_drawn_inputs = setup_inputs


def setup_inputs(seed=0):
    import zlib

    import numpy as np

    out = dict(_drawn_inputs(seed))
    spreads = {'L0_ffn_up_scale': (1.0, 0.2), 'L0_ffn_down_scale': (1.0, 0.2)}
    factors = {}
    for name, (base, spread) in spreads.items():
        noise = np.random.default_rng([zlib.crc32(name.encode()), seed]).standard_normal(out[name].shape)
        drawn = base * np.exp(spread * noise) if base else spread * noise
        out[name] = jnp.asarray(drawn.astype(out[name].dtype))
    for name, factor in factors.items():
        out[name] = (out[name] * factor).astype(out[name].dtype)
    return out
```

```python
import concourse.bass as bass
from concourse import mybir
from contextlib import ExitStack

P = 128
B, HW, K8 = 4, 128, 8
L = (HW // K8) ** 2
TOK = B * L
PIX = K8 * K8
C = 512
HD = 32
HID = 2048
CT = C // P
TT = TOK // P
TPB = L // P
ST = HID // P
CH = 4 * P
TPC = CH // P
NH = P // HD
G1 = P + NH
BIAS, ONE = 64, 96
LN_EPS = 1e-5
ATT_EPS = 1e-15


def vit_tower(nc, uf_t, uf_tok, blocks, blocks_t, w_qkv, w_proj, b_proj, w_up, w_down, up_scale, down_scale,
              out_scale, out):
    f32, f32r = mybir.dt.float32, mybir.dt.float32r
    ALU = mybir.AluOpType
    ACT = mybir.ActivationFunctionType

    with ExitStack() as ctx:
        def sb(name, shape, dt=f32):
            return ctx.enter_context(nc.sbuf_tensor(name, shape, dt))

        def early(*specs):
            with ExitStack() as short:
                return [short.enter_context(nc.sbuf_tensor(n, s, d)) for n, s, d in specs]

        def sem(name):
            return ctx.enter_context(nc.semaphore(name))

        w_sb, uf_raw, h_lhs = early(("w_sb", [P, CT, 3 * C], f32), ("uf_raw", [P, TOK], f32), ("h_lhs", [P, TOK], f32))
        up_raw = sb("up_raw", [P, CT, HID])
        q_hi, q_lo = early(("q_hi", [P, CT, TOK], f32r), ("q_lo", [P, CT, TOK], f32r))
        dn_raw = sb("dn_raw", [P, ST, C])
        k_hi, k_lo = early(("k_hi", [P, 4, C], f32r), ("k_lo", [P, 4, C], f32r))
        x2t0_hi, x2t0_lo = sb("x2t0_hi", [P, CT, CH], f32r), sb("x2t0_lo", [P, CT, CH], f32r)
        at_hi, at_lo = early(("at_hi", [P, 4, CT, P], f32r), ("at_lo", [P, 4, CT, P], f32r))
        x2t1_hi, x2t1_lo = sb("x2t1_hi", [P, CT, CH], f32r), sb("x2t1_lo", [P, CT, CH], f32r)
        u1, u2, ma, mb, xa, xa_hi, xa_lo = early(
            ("u1", [P, TOK], f32r), ("u2", [P, TOK], f32r), ("ma", [P, 2 * C], f32r), ("mb", [P, 2 * C], f32r),
            ("xa", [P, TT, P], f32), ("xa_hi", [P, TT, P], f32r), ("xa_lo", [P, TT, P], f32r))
        up_sgn, dn_sgn = sb("up_sgn", [P, 2, CT, P], f32r), sb("dn_sgn", [P, 2, C], f32r)
        hid, hid_hi, hid_lo = sb("hid", [P, 2, CH]), sb("hid_hi", [P, 2, CH], f32r), sb("hid_lo", [P, 2, CH], f32r)
        scaled = sb("scaled", [P, 2, C])
        rest = sb("rest", [P, 2, C])
        bt_raw, bt, ba, bc = early(("bt_raw", [P, C], f32), ("bt", [P, C], f32), ("ba", [P, CT, P], f32),
                                   ("bc", [P, CT, P], f32))
        g_hi, g_lo = sb("g_hi", [P, 2, C], f32r), sb("g_lo", [P, 2, C], f32r)
        (wp_raw,) = early(("wp_raw", [P, CT, C], f32))
        att, x2 = sb("att", [P, 2, C]), sb("x2", [P, 2, C])
        wp_hi, wp_lo = sb("wp_hi", [P, CT, C], f32r), sb("wp_lo", [P, CT, C], f32r)
        h_sb = sb("h_sb", [P, TT, C])
        v_hi, v_lo = sb("v_hi", [P, CT, G1], f32r), sb("v_lo", [P, CT, G1], f32r)
        vk = sb("vk", [P, CT, G1])
        vk_hi, vk_lo = sb("vk_hi", [P, 2, CT, G1], f32r), sb("vk_lo", [P, 2, CT, G1], f32r)
        blk = sb("blk", [P, CT, PIX])
        uft = sb("uft", [P, TT, PIX])
        sq_junk = sb("sq_junk", [P, TT, PIX])
        bp_b = sb("bp_b", [P, C])
        ds_b = sb("ds_b", [P, C])
        os_b = sb("os_b", [P, 1])
        us = sb("us", [P, ST])
        ident = sb("ident", [P, P])
        mean_w = sb("mean_w", [P, P])
        mask = sb("mask", [P, G1])
        sqb, sqa = sb("sqb", [P, CT]), sb("sqa", [P, TT])
        st1, mv1 = sb("st1", [P, TT, 6]), sb("mv1", [P, TT, 2])
        ve1, sd1, y1, t1, rs1, rr1, es1 = (sb(n, [P, TT]) for n in ("ve1", "sd1", "y1", "t1", "rs1", "rr1", "es1"))
        st2, mv2 = sb("st2", [P, TT, 6]), sb("mv2", [P, TT, 2])
        ve2, sd2, y2, t2, rs2 = (sb(n, [P, TT]) for n in ("ve2", "sd2", "y2", "t2", "rs2"))
        den, rden = sb("den", [P, 2, CT, NH]), sb("rden", [P, 2, CT, NH])

        ps = ctx.enter_context(nc.psum_tensor("ps", [P, 8, C], f32))

        ld_blk, ld_bt, ld_ufr, ld_hl, ld_uft = sem("ld_blk"), sem("ld_bt"), sem("ld_ufr"), sem("ld_hl"), sem("ld_uft")
        ld_w = [sem(f"ld_w{i}") for i in range(3)]
        ld_wp, ld_bp, ld_sc = sem("ld_wp"), sem("ld_bp"), sem("ld_sc")
        ld_up = [sem(f"ld_up{i}") for i in range(4)]
        ld_dn = [sem(f"ld_dn{i}") for i in range(4)]
        st_out = sem("st_out")
        ba_zero, meanw_set, hl_set, ident_0, ident_set = (
            sem("ba_zero"), sem("meanw_set"), sem("hl_set"), sem("ident_0"), sem("ident_set"))
        mask_0, mask_set, v_zero, v_one, mb_zero, xa_zero = (
            sem("mask_0"), sem("mask_set"), sem("v_zero"), sem("v_one"), sem("mb_zero"), sem("xa_zero"))
        u2_zero, u2_set = sem("u2_zero"), sem("u2_set")
        sqb_done, ba_done, ba_sq, mean_done, bc_done = (
            sem("sqb_done"), sem("ba_done"), sem("ba_sq"), sem("mean_done"), sem("bc_done"))
        bt_done, u1_hi, u2_hi, u1_lo, sqa_done = (
            sem("bt_done"), sem("u1_hi"), sem("u2_hi"), sem("u1_lo"), sem("sqa_done"))
        h_done, h_out, h_stat, h_bias = sem("h_done"), sem("h_out"), sem("h_stat"), sem("h_bias")
        ve1_done, sd1_done, xa_done = sem("ve1_done"), sem("sd1_done"), sem("xa_done")
        m_done, m_hi, m_lo, m_dup = sem("m_done"), sem("m_hi"), sem("m_lo"), sem("m_dup")
        kq_done, kq_hi, kq_lo = sem("kq_done"), sem("kq_hi"), sem("kq_lo")
        g_done, gh_done, gl_done = sem("g_done"), sem("gh_done"), sem("gl_done")
        vk_done, vk_full, vkh_done, vkl_done = sem("vk_done"), sem("vk_full"), sem("vkh_done"), sem("vkl_done")
        out_done, att_done = sem("out_done"), sem("att_done")
        t_done, th_done, tl_done = sem("t_done"), sem("th_done"), sem("tl_done")
        wph_done, wpl_done = sem("wph_done"), sem("wpl_done")
        proj_done, h2_done, ve2_done, sd2_done, rs2_done, x2_done = (
            sem("proj_done"), sem("h2_done"), sem("ve2_done"), sem("sd2_done"), sem("rs2_done"), sem("x2_done"))
        upsgn_done, dnsgn_done, up_done, dn_done = sem("upsgn_done"), sem("dnsgn_done"), sem("up_done"), sem("dn_done")
        relu_done, hidh_done, hidl_done, acc_done, fin_done = (
            sem("relu_done"), sem("hidh_done"), sem("hidl_done"), sem("acc_done"), sem("fin_done"))
        v_step = sem("v_step")

        order = [("kq", u) for u in range(8)]
        order += [("G", 0), ("kq", 8), ("G", 1), ("kq", 9), ("VK", 0), ("kq", 10), ("VK", 1), ("kq", 11)]
        order += [("kq", u) for u in range(12, 16)]
        order += [("out", 0), ("G", 2), ("out", 1), ("G", 3), ("aT", 0), ("out", 2), ("VK", 2), ("aT", 1), ("out", 3),
                  ("VK", 3), ("aT", 2), ("aT", 3), ("proj", 0), ("out", 4), ("proj", 1), ("ln", 0), ("out", 5),
                  ("aT", 4), ("proj", 2), ("xT", 0), ("ln", 1), ("out", 6), ("aT", 5), ("proj", 3), ("xT", 1),
                  ("ln", 2), ("out", 7), ("aT", 6), ("ln", 3), ("xT", 2), ("aT", 7), ("proj", 4), ("xT", 3),
                  ("proj", 5), ("ln", 4), ("proj", 6), ("ln", 5), ("proj", 7), ("ln", 6),
                  ("up", 0), ("xT", 4), ("up", 1), ("xT", 5), ("ln", 7), ("down", 0), ("up", 2), ("xT", 6),
                  ("down", 1), ("up", 3), ("xT", 7)]
        turns = {key: n for n, key in enumerate([key for key in order if key[0] in ("aT", "xT")])}
        acc_bank = [[2, 3, 6, 7], [4, 5, 2, 3]]
        g_cols = [slice(g * P, (g + 1) * P) for g in range(CT)]
        x2t = [(x2t0_hi, x2t0_lo), (x2t1_hi, x2t1_lo)]
        three = [(0, 0), (1, 0), (0, 1)]
        qs, vs, gs, vks, wps, ats, xas, ks = ((q_hi, q_lo), (v_hi, v_lo), (g_hi, g_lo), (vk_hi, vk_lo), (wp_hi, wp_lo),
                                              (at_hi, at_lo), (xa_hi, xa_lo), (k_hi, k_lo))

        def two_banks(first):
            return ps[:, first:first + 2, 0:2 * G1].rearrange("p a (g c) -> p a g c", g=2)

        block = ctx.enter_context(nc.Block())

        @block.sync
        def _(sp):
            b_v = blocks.rearrange("(t p) j -> p t j", p=P)
            w_v = w_qkv.rearrange("(t p) c -> p t c", p=P)
            sp.dma_start(blk[:], b_v).then_inc(ld_blk, 16)
            sp.dma_start(bt_raw[0:PIX, :], blocks_t).then_inc(ld_bt, 16)
            sp.dma_start(bt_raw[PIX:P, :], blocks_t).then_inc(ld_bt, 16)
            sp.dma_start(h_lhs[0:PIX, :], uf_t).then_inc(ld_hl, 16)
            sp.dma_start(uft[:], uf_tok).then_inc(ld_uft, 16)
            sp.dma_start(w_sb[:, :, C:2 * C], w_v[:, :, C:2 * C]).then_inc(ld_w[0], 16)
            sp.dma_start(uf_raw[0:PIX, :], uf_t).then_inc(ld_ufr, 16)
            sp.dma_start(uf_raw[PIX:P, :], uf_t).then_inc(ld_ufr, 16)
            sp.dma_start(w_sb[:, :, 0:C], w_v[:, :, 0:C]).then_inc(ld_w[1], 16)
            sp.dma_start(w_sb[:, :, 2 * C:3 * C], w_v[:, :, 2 * C:3 * C]).then_inc(ld_w[2], 16)
            sp.dma_start(bp_b[:], b_proj.to_broadcast([P, C])).then_inc(ld_bp, 16)
            sp.dma_start(wp_raw[:], w_proj.rearrange("(t p) c -> p t c", p=P)).then_inc(ld_wp, 16)
            sp.dma_start(ds_b[:], down_scale.to_broadcast([P, C])).then_inc(ld_sc, 16)
            sp.dma_start(os_b[:], out_scale.to_broadcast([P, 1])).then_inc(ld_sc, 16)
            sp.dma_start(us[:], up_scale).then_inc(ld_sc, 16)
            sp.wait_ge(m_done, 3)
            sp.wait_ge(h_done, TT)
            sp.wait_ge(u1_lo, 1)
            sp.wait_ge(u1_hi, 1)
            up_v = w_up.rearrange("(t p) c -> p t c", p=P)
            for i in range(4):
                cols = slice(i * HID // 4, (i + 1) * HID // 4)
                sp.dma_start(up_raw[:, :, cols], up_v[:, :, cols]).then_inc(ld_up[i], 16)
            sp.wait_ge(out_done, TT)
            dn_v = w_down.rearrange("(t p) c -> p t c", p=P)
            for i in range(4):
                rows = slice(i * ST // 4, (i + 1) * ST // 4)
                sp.dma_start(dn_raw[:, rows, :], dn_v[:, rows, :]).then_inc(ld_dn[i], 16)
            out_v = out.rearrange("(t p) c -> p t c", p=P)
            for t in range(TT):
                sp.wait_ge(fin_done, t + 1)
                sp.dma_start(out_v[:, t, :], h_sb[:, t, :]).then_inc(st_out, 16)
            sp.wait_ge(st_out, 16 * TT)

        @block.gpsimd
        def _(pool):
            nc.gpsimd.memset(ba[:], 0.0).then_inc(ba_zero, 1)
            pool.wait_ge(ba_zero, 1)
            nc.gpsimd.memset(mean_w[:], 1.0 / C).then_inc(meanw_set, 1)
            pool.wait_ge(meanw_set, 1)
            nc.gpsimd.memset(h_lhs[PIX:P, :], 1.0 / PIX).then_inc(hl_set, 1)
            pool.wait_ge(hl_set, 1)
            nc.gpsimd.memset(mb[ONE:P, :].bitcast(f32), 0.0).then_inc(mb_zero, 1)
            pool.wait_ge(mb_zero, 1)
            nc.gpsimd.memset(xa[:], 0.0).then_inc(xa_zero, 1)
            pool.wait_ge(xa_zero, 1)
            nc.gpsimd.memset(v_hi[:].bitcast(f32), 0.0).then_inc(v_zero, 1)
            pool.wait_ge(v_zero, 1)
            nc.gpsimd.memset(v_lo[:].bitcast(f32), 0.0).then_inc(v_zero, 1)
            pool.wait_ge(v_zero, 2)
            nc.gpsimd.memset(v_hi[ONE:ONE + 1, :, P:G1].bitcast(f32), 1.0).then_inc(v_one, 1)
            pool.wait_ge(v_one, 1)
            nc.gpsimd.memset(ident[:], 0.0).then_inc(ident_0, 1)
            pool.wait_ge(ident_0, 1)
            nc.gpsimd.affine_select(out=ident[:], in_=ident[:], compare_op=ALU.not_equal, fill=1.0, base=0,
                                    pattern=[[-1, P]], channel_multiplier=1).then_inc(ident_set, 1)
            pool.wait_ge(ident_set, 1)
            pool.wait_ge(u1_lo, 1)
            nc.gpsimd.memset(u2[PIX:P, :].bitcast(f32), 0.0).then_inc(u2_zero, 1)
            pool.wait_ge(u2_zero, 1)
            nc.gpsimd.memset(u2[BIAS:BIAS + 1, :].bitcast(f32), 1.0).then_inc(u2_set, 1)
            pool.wait_ge(u2_set, 1)
            nc.gpsimd.memset(u2[ONE:ONE + 1, :].bitcast(f32), 1.0).then_inc(u2_set, 1)
            pool.wait_ge(u2_set, 2)
            nc.gpsimd.memset(mask[:], 0.0).then_inc(mask_0, 1)
            pool.wait_ge(mask_0, 1)
            for h in range(NH):
                rows = slice(h * HD, (h + 1) * HD)
                nc.gpsimd.memset(mask[rows, rows], 1.0).then_inc(mask_set, 1)
                pool.wait_ge(mask_set, 2 * h + 1)
                nc.gpsimd.memset(mask[rows, P + h:P + h + 1], 1.0).then_inc(mask_set, 1)
                pool.wait_ge(mask_set, 2 * h + 2)
            pool.wait_ge(ld_wp, 16)
            nc.gpsimd.tensor_scalar(wp_hi[:], wp_raw[:], 1.0, None, ALU.mult).then_inc(wph_done, 1)
            pool.wait_ge(wph_done, 1)
            nc.gpsimd.tensor_tensor(wp_lo[:], wp_raw[:], wp_hi[:].bitcast(f32), ALU.subtract).then_inc(wpl_done, 1)
            pool.wait_ge(ld_bp, 16)

            def add_bias(t):
                pool.wait_ge(h_stat, t + 1)
                nc.gpsimd.tensor_tensor(h_sb[:, t, :], h_sb[:, t, :], bp_b[:], ALU.add).then_inc(h_bias, 1)

            for t in range(4):
                add_bias(t)
            for kind, i in order:
                if kind == "VK":
                    pool.wait_ge(vkh_done, i + 1)
                    if i >= 2:
                        pool.wait_ge(out_done, TPB * (i - 1))
                    nc.gpsimd.tensor_tensor(vk_lo[:, i % 2], vk[:], vk_hi[:, i % 2].bitcast(f32),
                                            ALU.subtract).then_inc(vkl_done, 1)
                    if i < 2:
                        add_bias(4 + 2 * i)
                        add_bias(5 + 2 * i)
                if kind == "ln":
                    pool.wait_ge(rs2_done, i + 1)
                    pool.wait_ge(wpl_done, 1)
                    if i >= 2:
                        pool.wait_ge(t_done, turns[("xT", i - 2)] + 1)
                    nc.gpsimd.tensor_scalar(x2[:, i % 2, :], h_sb[:, i, :], mv2[:, i, 0:1], rs2[:, i:i + 1],
                                            ALU.subtract, ALU.mult).then_inc(x2_done, 1)

        @block.scalar
        def _(act):
            act.wait_ge(ld_blk, 16)
            for t in range(CT):
                nc.scalar.activation(sq_junk[:, t, :], blk[:, t, :], ACT.Square, scale=1.0 / K8,
                                     accum_out=sqb[:, t:t + 1]).then_inc(sqb_done, 1)
            act.wait_ge(ba_zero, 1)
            nc.scalar.activation(ba[:, :, 0:PIX], blk[:], ACT.Copy, scale=-2.0 / PIX).then_inc(ba_done, 1)
            act.wait_ge(ld_bt, 32)
            nc.scalar.activation(bt[0:PIX, :], bt_raw[0:PIX, :], ACT.Copy, scale=-2.0 / PIX).then_inc(bt_done, 1)
            nc.scalar.activation(bt[PIX:P, :], bt_raw[PIX:P, :], ACT.Square).then_inc(bt_done, 1)
            act.wait_ge(ld_ufr, 32)
            nc.scalar.activation(u1[0:PIX, :], uf_raw[0:PIX, :], ACT.Copy).then_inc(u1_hi, 1)
            act.wait_ge(sqa_done, 1)
            for t in range(TT):
                act.wait_ge(h_done, t + 1)
                nc.scalar.activation(h_sb[:, t, :], ps[:, t % 3, :], ACT.Identity,
                                     bias=sqa[:, t:t + 1]).then_inc(h_out, 1)
            act.wait_ge(ve1_done, 1)
            nc.scalar.activation(sd1[:], ve1[:], ACT.Sqrt).then_inc(sd1_done, 1)
            for i in range(2):
                cols = slice(i * C, (i + 1) * C)
                act.wait_ge(m_done, i + 1)
                nc.scalar.activation(ma[0:ONE + 1, cols], ps[0:ONE + 1, 4 + i, :], ACT.Copy).then_inc(m_hi, 1)
                act.wait_ge(m_lo, i + 1)
                nc.scalar.activation(mb[BIAS:BIAS + 1, cols], ps[BIAS:BIAS + 1, 4 + i, :], ACT.Copy).then_inc(m_dup, 1)
                nc.scalar.activation(ma[PIX:P, cols], ps[0:PIX, 4 + i, :], ACT.Copy).then_inc(m_dup, 1)
            act.wait_ge(m_done, 3)
            act.wait_ge(v_zero, 2)
            nc.scalar.activation(v_hi[0:BIAS + 1, :, 0:P], ps[0:BIAS + 1, 6, :].rearrange("p (g c) -> p g c", g=CT),
                                 ACT.Copy).then_inc(m_hi, 1)

            def sign_up(step, c):
                nc.scalar.activation(up_sgn[:, step % 2], up_raw[:, :, bass.ds(c * P, P)], ACT.Sign).then_inc(upsgn_done, 1)

            def sign_down(step, c):
                nc.scalar.activation(dn_sgn[:, step % 2], dn_raw[:, c, :], ACT.Sign).then_inc(dnsgn_done, 1)

            def relu(step, c, wait):
                act.wait_ge(up_done, wait)
                nc.scalar.activation(hid[:, step % 2, :], ps[:, step % 2, :], ACT.Relu,
                                     scale=us[:, bass.ds(c, 1)]).then_inc(relu_done, 1)

            for kind, i in order:
                if kind == "kq":
                    act.wait_ge(kq_done, i + 1)
                    if i % 8 < 4:
                        t = i % 8 + 4 * (i // 8)
                        if t >= 4:
                            act.wait_ge(g_done, (t - 4) // TPB + 1)
                        dst = k_hi[:, t % 4, :]
                    else:
                        dst = q_hi[:, i % 4, (i // 8) * CH:(i // 8 + 1) * CH]
                    nc.scalar.activation(dst, ps[:, i % 4, :], ACT.Relu).then_inc(kq_hi, 1)
                elif kind == "G":
                    act.wait_ge(g_done, i + 1)
                    if i >= 2:
                        act.wait_ge(vk_done, i - 1)
                    nc.scalar.activation(g_hi[:, i % 2, :], ps[:, 4 + i % 2, :], ACT.Copy).then_inc(gh_done, 1)
                elif kind == "VK":
                    act.wait_ge(vk_full, i + 1)
                    if i >= 2:
                        act.wait_ge(out_done, TPB * (i - 1))
                    nc.scalar.activation(vk_hi[:, i % 2], vk[:], ACT.Copy).then_inc(vkh_done, 1)
                elif kind in ("aT", "xT"):
                    n = turns[(kind, i)]
                    act.wait_ge(t_done, n + 1)
                    src = ps[:, 4 + n % 2, :].rearrange("p (g c) -> p g c", g=CT)
                    if kind == "aT":
                        if i >= 4:
                            act.wait_ge(proj_done, i - 3)
                        dst = at_hi[:, i % 4]
                    else:
                        if i < TPC:
                            act.wait_ge(g_done, B)
                        else:
                            act.wait_ge(proj_done, TT)
                        dst = x2t[i // TPC][0][:, :, (i % TPC) * P:(i % TPC + 1) * P]
                    nc.scalar.activation(dst, src, ACT.Copy).then_inc(th_done, 1)
                elif kind == "proj":
                    act.wait_ge(ve2_done, i + 1)
                    nc.scalar.activation(sd2[:, i:i + 1], ve2[:, i:i + 1], ACT.Sqrt).then_inc(sd2_done, 1)
                    if i == 3:
                        act.wait_ge(g_done, B)
                        act.wait_ge(kq_done, 16)
                        act.wait_ge(ld_up[0], 16)
                        sign_up(0, 0)
                        sign_up(1, 1)
                    if i == 6:
                        act.wait_ge(ld_sc, 48)
                        act.wait_ge(ld_dn[0], 16)
                        sign_down(0, 0)
                elif kind == "up":
                    relu(i, i, i + 1)
                    sign_up(i + 2, i + 2)
                elif kind == "down":
                    if i >= 1:
                        act.wait_ge(dn_done, i)
                    sign_down(i + 1, i + 1)
            for i in range(1, 4):
                act.wait_ge(ld_up[i], 16)
                act.wait_ge(ld_dn[i], 16)

            def step_pair(s, first, ahead=2):
                for d in range(2):
                    act.wait_ge(dn_done, first + s + d)
                    sign_down(d + 1, s + d + 1)
                    relu(d, s + d + 2, first + s + d + 3)
                    if d < ahead:
                        sign_up(d, s + d + 4)

            for first in (0, ST):
                with act.Fori(1, ST // 2 - 2) as pair:
                    step_pair(2 * pair, first)
                step_12 = ST - 4
                for d in range(2):
                    act.wait_ge(dn_done, first + step_12 + d)
                    sign_down(d + 1, step_12 + d + 1)
                    relu(d, step_12 + d + 2, first + step_12 + d + 3)
                    if first == 0:
                        sign_up(d, d)
                if first == 0:
                    for s in range(4):
                        down = ST - 2 + s
                        act.wait_ge(dn_done, down)
                        sign_down(down + 1, (down + 1) % ST)
                        relu(s, s, ST + s + 1)
                        sign_up(s, s + 2)
                else:
                    act.wait_ge(dn_done, 2 * ST - 2)
                    sign_down(1, ST - 1)

        @block.vector
        def _(dve):
            steps = [0]

            def chain(ins):
                steps[0] += 1
                ins.then_inc(v_step, 1)
                dve.wait_ge(v_step, steps[0])

            def rsqrt(y, t, ve, sd, rs):
                chain(nc.vector.reciprocal(y, sd))
                chain(nc.vector.tensor_tensor(t, y, y, ALU.mult))
                chain(nc.vector.tensor_tensor(t, t, ve, ALU.mult))
                chain(nc.vector.tensor_scalar(t, t, -0.5, 1.5, ALU.mult, ALU.add))
                return nc.vector.tensor_tensor(rs, y, t, ALU.mult)

            dve.wait_ge(sqb_done, CT)
            dve.wait_ge(ba_zero, 1)
            for col in (BIAS, ONE):
                nc.vector.tensor_copy(ba[:, :, col], sqb[:]).then_inc(ba_sq, 1)
            dve.wait_ge(ld_uft, 16)
            dve.wait_ge(sqb_done, CT)
            chain(nc.vector.scalar_tensor_tensor(sq_junk[:], uft[:], 1.0 / PIX, uft[:], op0=ALU.mult, op1=ALU.mult))
            nc.vector.reduce_sum(sqa[:], sq_junk[:], mybir.AxisListType.X).then_inc(sqa_done, 1)
            dve.wait_ge(mean_done, 1)
            nc.vector.tensor_tensor(bc[:], ba[:], ps[:, 7, 0:P].unsqueeze(1).to_broadcast([P, CT, P]),
                                    ALU.subtract).then_inc(bc_done, 1)
            dve.wait_ge(ld_ufr, 32)
            nc.vector.tensor_copy(u2[:], uf_raw[:]).then_inc(u2_hi, 1)
            dve.wait_ge(u2_hi, 1)
            nc.vector.tensor_tensor(u1[PIX:P, :], uf_raw[PIX:P, :], u2[PIX:P, :].bitcast(f32),
                                    ALU.subtract).then_inc(u1_lo, 1)
            for t in range(TT):
                dve.wait_ge(h_out, t + 1)
                nc.vector.bn_stats(st1[:, t, :], h_sb[:, t, :]).then_inc(h_stat, 1)
            dve.wait_ge(h_stat, TT)
            for t in range(TT):
                last = nc.vector.bn_aggr(mv1[:, t, :], st1[:, t, :])
            chain(last)
            nc.vector.tensor_scalar(ve1[:], mv1[:, :, 1], LN_EPS, None, ALU.add).then_inc(ve1_done, 1)
            def m_low(i):
                dve.wait_ge(m_hi, i + 1)
                dve.wait_ge(mb_zero, 1)
                cols = slice(i * C, (i + 1) * C)
                nc.vector.tensor_tensor(mb[0:ONE + 1, cols], ps[0:ONE + 1, 4 + i, :], ma[0:ONE + 1, cols].bitcast(f32),
                                        ALU.subtract).then_inc(m_lo, 1)

            m_low(0)
            dve.wait_ge(sd1_done, 1)
            dve.wait_ge(ve1_done, 1)
            chain(rsqrt(y1[:], t1[:], ve1[:], sd1[:], rs1[:]))
            chain(nc.vector.tensor_tensor(rr1[:], rs1[:], rs1[:], ALU.mult))
            dve.wait_ge(xa_zero, 1)
            nc.vector.tensor_tensor(xa[:, :, 0:PIX], uft[:], rr1[:].unsqueeze(2).to_broadcast([P, TT, PIX]), ALU.mult)
            nc.vector.tensor_copy(xa[:, :, BIAS], rr1[:])
            chain(nc.vector.tensor_copy(xa[:, :, ONE], rs1[:]))
            nc.vector.scalar_tensor_tensor(es1[:], ve1[:], ATT_EPS, rs1[:], op0=ALU.mult, op1=ALU.mult)
            m_low(1)
            chain(nc.vector.tensor_copy(xa_hi[:], xa[:]))
            nc.vector.tensor_tensor(xa_lo[:], xa[:], xa_hi[:].bitcast(f32), ALU.subtract).then_inc(xa_done, 1)
            dve.wait_ge(m_hi, 3)
            nc.vector.tensor_tensor(v_lo[0:BIAS + 1, :, 0:P], ps[0:BIAS + 1, 6, :].rearrange("p (g c) -> p g c", g=CT),
                                    v_hi[0:BIAS + 1, :, 0:P].bitcast(f32), ALU.subtract).then_inc(m_lo, 1)

            def hidden(slot, relu_wait, hi_wait):
                dve.wait_ge(relu_done, relu_wait)
                nc.vector.tensor_copy(hid_hi[:, slot, :], hid[:, slot, :]).then_inc(hidh_done, 1)
                dve.wait_ge(hidh_done, hi_wait)
                nc.vector.tensor_tensor(hid_lo[:, slot, :], hid[:, slot, :], hid_hi[:, slot, :].bitcast(f32),
                                        ALU.subtract).then_inc(hidl_done, 1)

            def finish(chunk, i):
                t = chunk * TPC + i
                dve.wait_ge(acc_done, t + 1)
                if t == 0:
                    dve.wait_ge(ld_sc, 48)
                chain(nc.vector.tensor_tensor(scaled[:, i % 2, :], ps[:, acc_bank[chunk][i], :], ds_b[:], ALU.mult))
                nc.vector.scalar_tensor_tensor(h_sb[:, t, :], scaled[:, i % 2, :], os_b[:, 0:1], h_sb[:, t, :],
                                               op0=ALU.mult, op1=ALU.add).then_inc(fin_done, 1)

            for kind, i in order:
                if kind == "kq":
                    dve.wait_ge(kq_hi, i + 1)
                    if i % 8 < 4:
                        t = i % 8 + 4 * (i // 8)
                        dst, hi = k_lo[:, t % 4, :], k_hi[:, t % 4, :]
                    else:
                        cols = slice((i // 8) * CH, (i // 8 + 1) * CH)
                        dst, hi = q_lo[:, i % 4, cols], q_hi[:, i % 4, cols]
                    nc.vector.scalar_tensor_tensor(dst, ps[:, i % 4, :], 0.0, hi.bitcast(f32), op0=ALU.max,
                                                   op1=ALU.subtract).then_inc(kq_lo, 1)
                elif kind == "G":
                    dve.wait_ge(gh_done, i + 1)
                    nc.vector.tensor_tensor(g_lo[:, i % 2, :], ps[:, 4 + i % 2, :], g_hi[:, i % 2, :].bitcast(f32),
                                            ALU.subtract).then_inc(gl_done, 1)
                elif kind == "VK":
                    dve.wait_ge(vk_done, i + 1)
                    if i == 0:
                        dve.wait_ge(mask_set, 2 * NH)
                    else:
                        dve.wait_ge(vkl_done, i)
                    nc.vector.tensor_tensor(vk[:].rearrange("p (a g) c -> p a g c", a=2), two_banks(6),
                                            mask[:].unsqueeze(1).unsqueeze(1).to_broadcast([P, 2, 2, G1]),
                                            ALU.mult).then_inc(vk_full, 1)
                elif kind == "out":
                    dve.wait_ge(out_done, i + 1)
                    if i == 0:
                        dve.wait_ge(wpl_done, 1)
                    else:
                        dve.wait_ge(att_done, 2 * i)
                    o = two_banks(2 * (i % 2))
                    for a in range(2):
                        last = nc.vector.tensor_scalar(den[:, i % 2, 2 * a:2 * a + 2, :], o[:, a, :, P:G1],
                                                       es1[:, i:i + 1], None, ALU.add)
                    chain(last)
                    chain(nc.vector.reciprocal(rden[:, i % 2], den[:, i % 2]))
                    if i >= 2:
                        dve.wait_ge(t_done, turns[("aT", i - 2)] + 1)
                    for a in range(2):
                        nc.vector.tensor_tensor(
                            att[:, i % 2, a * 2 * P:(a + 1) * 2 * P].rearrange("p (g h d) -> p g h d", g=2, h=NH),
                            o[:, a, :, 0:P].rearrange("p g (h d) -> p g h d", h=NH),
                            rden[:, i % 2, 2 * a:2 * a + 2, :].unsqueeze(3).to_broadcast([P, 2, NH, HD]),
                            ALU.mult).then_inc(att_done, 1)
                elif kind in ("aT", "xT"):
                    n = turns[(kind, i)]
                    dve.wait_ge(th_done, n + 1)
                    src = ps[:, 4 + n % 2, :].rearrange("p (g c) -> p g c", g=CT)
                    if kind == "aT":
                        dst, hi = at_lo[:, i % 4], at_hi[:, i % 4]
                    else:
                        cols = slice((i % TPC) * P, (i % TPC + 1) * P)
                        dst, hi = x2t[i // TPC][1][:, :, cols], x2t[i // TPC][0][:, :, cols]
                    nc.vector.tensor_tensor(dst, src, hi.bitcast(f32), ALU.subtract).then_inc(tl_done, 1)
                elif kind == "proj":
                    dve.wait_ge(proj_done, i + 1)
                    dve.wait_ge(h_bias, i + 1)
                    nc.vector.tensor_tensor(h_sb[:, i, :], ps[:, 6 + i % 2, :], h_sb[:, i, :],
                                            ALU.add).then_inc(h2_done, 1)
                    dve.wait_ge(h2_done, i + 1)
                    chain(nc.vector.bn_stats(st2[:, i, :], h_sb[:, i, :]))
                    chain(nc.vector.bn_aggr(mv2[:, i, :], st2[:, i, :]))
                    nc.vector.tensor_scalar(ve2[:, i:i + 1], mv2[:, i, 1:2], LN_EPS, None,
                                            ALU.add).then_inc(ve2_done, 1)
                elif kind == "ln":
                    dve.wait_ge(sd2_done, i + 1)
                    one = slice(i, i + 1)
                    rsqrt(y2[:, one], t2[:, one], ve2[:, one], sd2[:, one], rs2[:, one]).then_inc(rs2_done, 1)
                elif kind == "up":
                    if i >= 2:
                        dve.wait_ge(dn_done, i - 1)
                    hidden(i % 2, i + 1, i + 1)

            for chunk in range(2):
                first = chunk * ST
                with dve.Fori(1, ST // 2 - 1) as pair:
                    s = 2 * pair
                    for d in range(2):
                        dve.wait_ge(dn_done, first + s + d + 1)
                        hidden(d, first + s + d + 3, first + s + d + 3)
                if chunk == 0:
                    for s in range(4):
                        dve.wait_ge(dn_done, ST + s - 1)
                        hidden(s % 2, ST + s + 1, ST + s + 1)
                        if s < 2:
                            finish(0, 2 * s)
                            finish(0, 2 * s + 1)
                else:
                    for i in range(TPC):
                        finish(1, i)

        @block.tensor
        def _(pe):
            mm = nc.tensor.matmul
            pe.wait_ge(meanw_set, 1)
            pe.wait_ge(ba_done, 1)
            pe.wait_ge(ba_sq, 2)
            for t in range(CT):
                last = mm(ps[:, 7, 0:P], mean_w[:], ba[:, t, :], start=(t == 0), stop=(t == CT - 1))
            last.then_inc(mean_done, 1)
            pe.wait_ge(bt_done, 2)
            pe.wait_ge(ld_hl, 16)
            pe.wait_ge(hl_set, 1)
            for t in range(TT):
                if t >= 3:
                    pe.wait_ge(h_out, t - 2)
                mm(ps[:, t % 3, :], h_lhs[:, t * P:(t + 1) * P], bt[:], start=True, stop=True).then_inc(h_done, 1)
            pe.wait_ge(bc_done, 1)
            for i, col in enumerate((C, 0, 2 * C)):
                pe.wait_ge(ld_w[i], 16)
                for t in range(CT):
                    last = mm(ps[:, 4 + i, :], bc[:, t, :], w_sb[:, t, col:col + C], start=(t == 0), stop=(t == CT - 1))
                last.then_inc(m_done, 1)

            def up(step, chunk, wait):
                pe.wait_ge(upsgn_done, wait)
                for part in range(2):
                    for t in range(CT):
                        last = mm(ps[:, step % 2, :], up_sgn[:, step % 2, t, :], x2t[chunk][part][:, t, :],
                                  start=(part == 0 and t == 0), stop=(part == 1 and t == CT - 1))
                last.then_inc(up_done, 1)

            def down(step, chunk, wait, begin=False, end=False):
                pe.wait_ge(dnsgn_done, wait)
                pe.wait_ge(hidl_done, wait)
                for i in range(TPC):
                    if begin and chunk == 1 and i == 2:
                        pe.wait_ge(fin_done, 1)
                    if begin and chunk == 1 and i == 3:
                        pe.wait_ge(fin_done, 2)
                    for part, half in enumerate((hid_hi, hid_lo)):
                        last = mm(ps[:, acc_bank[chunk][i], :], half[:, step % 2, i * P:(i + 1) * P],
                                  dn_sgn[:, step % 2, :], start=(begin and part == 0), stop=(end and part == 1))
                    if end:
                        last.then_inc(acc_done, 1)
                if not end:
                    last.then_inc(dn_done, 1)

            for kind, i in order:
                if kind == "kq":
                    if i < 4:
                        pe.wait_ge(h_out, TT)
                    else:
                        pe.wait_ge(kq_lo, i - 3)
                    if i == 0:
                        pe.wait_ge(u1_hi, 1)
                        pe.wait_ge(u1_lo, 1)
                        pe.wait_ge(u2_set, 2)
                    is_k = i % 8 < 4
                    if i in (0, 4):
                        pe.wait_ge(m_dup, 2 if is_k else 4)
                    if is_k:
                        t = i % 8 + 4 * (i // 8)
                        cols = slice(t * P, (t + 1) * P)
                        mm(ps[:, i % 4, :], u1[:, cols], ma[:, 0:C], start=True, stop=False)
                        mm(ps[:, i % 4, :], u2[:, cols], mb[:, 0:C], start=False, stop=True).then_inc(kq_done, 1)
                    else:
                        chans = slice(C + (i % 4) * P, C + (i % 4 + 1) * P)
                        cols = slice((i // 8) * CH, (i // 8 + 1) * CH)
                        mm(ps[:, i % 4, :], ma[:, chans], u1[:, cols], start=True, stop=False)
                        mm(ps[:, i % 4, :], mb[:, chans], u2[:, cols], start=False, stop=True).then_inc(kq_done, 1)
                elif kind == "G":
                    if i == 0:
                        pe.wait_ge(xa_done, 1)
                        pe.wait_ge(m_dup, 4)
                    if i >= 2:
                        pe.wait_ge(gl_done, i - 1)
                    pe.wait_ge(kq_lo, (2, 4, 10, 12)[i])
                    for n in range(TPB):
                        t = i * TPB + n
                        for j, (a, b) in enumerate(three):
                            last = mm(ps[:, 4 + i % 2, :], xas[a][:, t, :], ks[b][:, t % 4, :],
                                      start=(n == 0 and j == 0), stop=(n == TPB - 1 and j == 2))
                    last.then_inc(g_done, 1)
                elif kind == "VK":
                    if i == 0:
                        pe.wait_ge(m_lo, 3)
                        pe.wait_ge(v_one, 1)
                        pe.wait_ge(bc_done, 1)
                    else:
                        pe.wait_ge(vk_full, i)
                    pe.wait_ge(gl_done, i + 1)
                    o = two_banks(6)
                    for g in range(CT):
                        for j, (a, b) in enumerate(three):
                            last = mm(o[:, g // 2, g % 2, :], gs[a][:, i % 2, g_cols[g]], vs[b][:, g, :],
                                      start=(j == 0), stop=(j == 2))
                    last.then_inc(vk_done, 1)
                elif kind == "out":
                    b_i = i // TPB
                    pe.wait_ge(vkl_done, b_i + 1)
                    if i < 2:
                        pe.wait_ge(kq_lo, 14 + 2 * i)
                    else:
                        pe.wait_ge(att_done, 2 * (i - 1))
                    o = two_banks(2 * (i % 2))
                    for g in range(CT):
                        for j, (a, b) in enumerate(three):
                            last = mm(o[:, g // 2, g % 2, :], qs[a][:, g, i * P:(i + 1) * P], vks[b][:, b_i % 2, g, :],
                                      start=(j == 0), stop=(j == 2))
                    last.then_inc(out_done, 1)
                elif kind in ("aT", "xT"):
                    n = turns[(kind, i)]
                    if n < 2:
                        pe.wait_ge(gl_done, 3 + n)
                    else:
                        pe.wait_ge(tl_done, n - 1)
                    if kind == "aT":
                        pe.wait_ge(att_done, 2 * (i + 1))
                        pe.wait_ge(ident_set, 1)
                        src = att[:, i % 2, :]
                    else:
                        pe.wait_ge(x2_done, i + 1)
                        src = x2[:, i % 2, :]
                    for g in range(CT):
                        last = nc.tensor.transpose(ps[:, 4 + n % 2, g_cols[g]], src[:, g_cols[g]], ident[:])
                    last.then_inc(t_done, 1)
                elif kind == "proj":
                    if i < 2:
                        pe.wait_ge(vk_full, B)
                        pe.wait_ge(wpl_done, 1)
                    else:
                        pe.wait_ge(h2_done, i - 1)
                    pe.wait_ge(tl_done, turns[("aT", i)] + 1)
                    for g in range(CT):
                        for j, (a, b) in enumerate(three):
                            last = mm(ps[:, 6 + i % 2, :], ats[a][:, i % 4, g, :], wps[b][:, g, :],
                                      start=(g == 0 and j == 0), stop=(g == CT - 1 and j == 2))
                    last.then_inc(proj_done, 1)
                elif kind == "up":
                    if i < 2:
                        pe.wait_ge(att_done, 2 * TT)
                        pe.wait_ge(tl_done, turns[("xT", TPC - 1)] + 1)
                    else:
                        pe.wait_ge(relu_done, i - 1)
                    up(i, 0, i + 1)
                elif kind == "down":
                    if i == 0:
                        pe.wait_ge(h2_done, TT)
                    down(i, 0, i + 1, begin=(i == 0))
            for chunk in range(2):
                first = chunk * ST
                with pe.Fori(1, ST // 2 - 1) as pair:
                    s = 2 * pair
                    for d in range(2):
                        down(d, chunk, first + s + d + 1)
                        pe.wait_ge(relu_done, first + s + d + 1)
                        up(d, chunk, first + s + d + 3)
                if chunk == 0:
                    pe.wait_ge(tl_done, len(turns))
                    for n in range(4):
                        step = ST - 2 + n
                        down(step, step // ST, step + 1, begin=(step == ST), end=(step == ST - 1))
                        pe.wait_ge(relu_done, ST + n - 1)
                        up(n, 1, ST + n + 1)
                else:
                    down(0, 1, 2 * ST - 1)
                    down(1, 1, 2 * ST, end=True)


def kernel(x, L0_tok_blocks, L0_attn_w_qkv, L0_attn_w_proj, L0_attn_b_proj, L0_ffn_up_weight, L0_ffn_down_weight,
           L0_ffn_up_scale, L0_ffn_down_scale, L0_ffn_output_scale):
    import numpy as np
    import concourse.bacc as bacc
    from concourse.bass_utils import run_bass_kernel_spmd

    x = np.asarray(x)
    n = HW // K8
    patches = x.reshape(B, n, K8, n, K8)
    uf_t = patches.transpose(2, 4, 0, 1, 3).reshape(PIX, TOK)
    uf_tok = patches.transpose(0, 1, 3, 2, 4).reshape(TT, P, PIX).transpose(1, 0, 2)
    arrays = {
        "uf_t": uf_t,
        "uf_tok": uf_tok,
        "blocks": np.asarray(L0_tok_blocks),
        "blocks_t": np.asarray(L0_tok_blocks).T,
        "w_qkv": np.asarray(L0_attn_w_qkv).T,
        "w_proj": np.asarray(L0_attn_w_proj).T,
        "b_proj": np.asarray(L0_attn_b_proj).reshape(1, C),
        "w_up": np.asarray(L0_ffn_up_weight).T,
        "w_down": np.asarray(L0_ffn_down_weight).T,
        "up_scale": np.asarray(L0_ffn_up_scale).reshape(ST, P).T,
        "down_scale": np.asarray(L0_ffn_down_scale).reshape(1, C),
        "out_scale": np.asarray(L0_ffn_output_scale).reshape(1, 1),
    }
    arrays = {k: np.ascontiguousarray(v) for k, v in arrays.items()}
    nc = bacc.Bacc("TRN2", target_bir_lowering=False, num_devices=1)
    ins = [nc.dram_tensor(k, v.shape, mybir.dt.float32, kind="ExternalInput").ap() for k, v in arrays.items()]
    out = nc.dram_tensor("out", (TOK, C), mybir.dt.float32, kind="ExternalOutput").ap()
    vit_tower(nc, *ins, out)
    r = run_bass_kernel_spmd(nc, [arrays], core_ids=[0])
    return np.asarray(r.results[0]["out"]).reshape(B, L, C)
```

```python
import concourse.bass as bass
from concourse import mybir
from contextlib import ExitStack

P = 128
B, HW, K8 = 4, 128, 8
L = (HW // K8) ** 2
TOK = B * L
PIX = K8 * K8
C = 512
HD = 32
HID = 2048
CT = C // P
TT = TOK // P
TPB = L // P
ST = HID // P
CH = 4 * P
TPC = CH // P
NH = P // HD
G1 = P + NH
BIAS, ONE = 64, 96
XW = ONE + 2
HALF = 0.5
WARM = 8
LN_EPS = 1e-5
ATT_EPS = 1e-15


def vit_tower(nc, uf_t, uf_tok, blocks, blocks_t, w_qkv, w_proj, b_proj, w_up, w_down, up_scale, down_scale,
              out_scale, out):
    f32, f32r = mybir.dt.float32, mybir.dt.float32r
    ALU = mybir.AluOpType
    ACT = mybir.ActivationFunctionType

    with ExitStack() as ctx:
        def sb(name, shape, dt=f32):
            return ctx.enter_context(nc.sbuf_tensor(name, shape, dt))

        def early(*specs):
            with ExitStack() as short:
                return [short.enter_context(nc.sbuf_tensor(n, s, d)) for n, s, d in specs]

        def sem(name):
            return ctx.enter_context(nc.semaphore(name))

        w_sb, uf_raw = early(("w_sb", [P, CT, 3 * C], f32), ("uf_raw", [P, TOK], f32))
        up_raw = sb("up_raw", [P, CT, HID])
        k_hi, k_lo, bt, ba, bc = early(("k_hi", [P, 4, C], f32r), ("k_lo", [P, 4, C], f32r), ("bt", [P, C], f32),
                                       ("ba", [P, CT, P], f32), ("bc", [P, CT, P], f32))
        k_again, g_hi, g_lo, blk, uft, sq_junk = early(
            ("k_again", [P, 2, 4, C], f32), ("g_hi", [P, 2, C], f32r), ("g_lo", [P, 2, C], f32r),
            ("blk", [P, CT, PIX], f32), ("uft", [P, TT, PIX], f32), ("sq_junk", [P, TT, PIX], f32))
        _, _, kq_full = early(("k_too", [P, 2, 4, C], f32), ("g_too", [P, 4, C], f32), ("kq_full", [P, 2, C], f32))
        dn_raw = sb("dn_raw", [P, ST, C])
        q0_hi, q0_lo = early(("q0_hi", [P, CT, CH], f32r), ("q0_lo", [P, CT, CH], f32r))
        x2t1_hi, x2t1_lo = sb("x2t1_hi", [P, CT, CH], f32r), sb("x2t1_lo", [P, CT, CH], f32r)
        ha, hb = early(("ha", [P, C], f32r), ("hb", [P, C], f32r))
        q1_hi, q1_lo = sb("q1_hi", [P, CT, CH], f32r), sb("q1_lo", [P, CT, CH], f32r)
        x2t0_hi, x2t0_lo = sb("x2t0_hi", [P, CT, CH], f32r), sb("x2t0_lo", [P, CT, CH], f32r)
        u1, u2, ma, mb, xa, xa_hi, xa_lo = early(
            ("u1", [P, TOK], f32r), ("u2", [P, TOK], f32r), ("ma", [P, 2 * C], f32r), ("mb", [P, 2 * C], f32r),
            ("xa", [P, TT, XW], f32), ("xa_hi", [P, TT, XW], f32r), ("xa_lo", [P, TT, XW], f32r))
        x2 = sb("x2", [P, 2, C])
        up_sgn, dn_sgn = sb("up_sgn", [P, 2, CT, P], f32r), sb("dn_sgn", [P, 2, C], f32r)
        hid, hid_hi, hid_lo = sb("hid", [P, 2, CH]), sb("hid_hi", [P, 2, CH], f32r), sb("hid_lo", [P, 2, CH], f32r)
        scaled = sb("scaled", [P, 2, C])
        (wp_raw,) = early(("wp_raw", [P, CT, C], f32))
        att, at_hi = sb("att", [P, 2, C]), sb("at_hi", [P, 2, CT, P], f32r)
        wp_hi, wp_lo = sb("wp_hi", [P, CT, C], f32r), sb("wp_lo", [P, CT, C], f32r)
        at_lo = sb("at_lo", [P, 2, CT, P], f32r)
        h_sb = sb("h_sb", [P, TT, C])
        v_hi, v_lo = sb("v_hi", [P, CT, G1], f32r), sb("v_lo", [P, CT, G1], f32r)
        vk = sb("vk", [P, CT, G1])
        vk_hi, vk_lo = sb("vk_hi", [P, 2, CT, G1], f32r), sb("vk_lo", [P, 2, CT, G1], f32r)
        (bp_b,) = early(("bp_b", [P, C], f32))
        ds_b = sb("ds_b", [P, C])
        eps = sb("eps", [P, 1])
        t_copy = sb("t_copy", [P, 2, C])
        os_b = sb("os_b", [P, 1])
        us = sb("us", [P, ST])
        ident = sb("ident", [P, P])
        mean_w = sb("mean_w", [P, P])
        pick = sb("pick", [P, P])
        mask = sb("mask", [P, G1])
        sqa = sb("sqa", [P, TT])
        shift, sd0 = sb("shift", [P, 2]), sb("sd0", [P, 1])
        st1, mv1 = sb("st1", [P, TT, 6]), sb("mv1", [P, TT, 2])
        ve1, sd1, y1, t1, rs1, rr1, es1 = (sb(n, [P, TT]) for n in ("ve1", "sd1", "y1", "t1", "rs1", "rr1", "es1"))
        st2, mv2 = sb("st2", [P, TT, 6]), sb("mv2", [P, TT, 2])
        sd2, y2, t2, rs2 = (sb(n, [P, TT]) for n in ("sd2", "y2", "t2", "rs2"))
        den, rden = sb("den", [P, 2, CT, NH]), sb("rden", [P, 2, CT, NH])

        ps = ctx.enter_context(nc.psum_tensor("ps", [P, 8, C], f32))

        ld_blk, ld_bt, ld_sq, ld_uf, ld_uft = sem("ld_blk"), sem("ld_bt"), sem("ld_sq"), sem("ld_uf"), sem("ld_uft")
        ld_w = [sem(f"ld_w{i}") for i in range(6)]
        ld_wp, ld_bp, ld_os, ld_ds = sem("ld_wp"), sem("ld_bp"), sem("ld_os"), sem("ld_ds")
        ld_up = [sem(f"ld_up{i}") for i in range(4)]
        ld_dn = [sem(f"ld_dn{i}") for i in range(4)]
        st_out = sem("st_out")
        ba_zero, shift_set, meanw_set, pick_0, pick_1, pick_set, ident_0, ident_set = (
            sem("ba_zero"), sem("shift_set"), sem("meanw_set"), sem("pick_0"), sem("pick_1"), sem("pick_set"),
            sem("ident_0"), sem("ident_set"))
        mask_0, mask_set, v_zero, v_one, mb_zero, hb_zero, xa_zero, u2_zero, u2_set, ds_done = (
            sem("mask_0"), sem("mask_set"), sem("v_zero"), sem("v_one"), sem("mb_zero"), sem("hb_zero"),
            sem("xa_zero"), sem("u2_zero"), sem("u2_set"), sem("ds_done"))
        eps_set = sem("eps_set")
        sqb_done, ba_done, ba_sq, mean_done, bc_done = (
            sem("sqb_done"), sem("ba_done"), sem("ba_sq"), sem("mean_done"), sem("bc_done"))
        bt_done, hp_done, hp_hi, hp_lo, hp_dup = (
            sem("bt_done"), sem("hp_done"), sem("hp_hi"), sem("hp_lo"), sem("hp_dup"))
        u1_hi, u2_hi, u1_lo, sqa_done = sem("u1_hi"), sem("u2_hi"), sem("u1_lo"), sem("sqa_done")
        bt_mid, uft_mid = sem("bt_mid"), sem("uft_mid")
        h_done, h_out, h_stat, h_bias = sem("h_done"), sem("h_out"), sem("h_stat"), sem("h_bias")
        ve1_done, sd1_done, xa_done = sem("ve1_done"), sem("sd1_done"), sem("xa_done")
        m_done, m_hi, m_lo, m_dup, vh_done, vl_done = (
            sem("m_done"), sem("m_hi"), sem("m_lo"), sem("m_dup"), sem("vh_done"), sem("vl_done"))
        kq_done, kq_hi, kq_lo = sem("kq_done"), sem("kq_hi"), sem("kq_lo")
        kq_copy, kq_plo = sem("kq_copy"), sem("kq_plo")
        g_done, gh_done, gl_done = sem("g_done"), sem("gh_done"), sem("gl_done")
        vk_done, vk_full, vkh_done, vkl_done = sem("vk_done"), sem("vk_full"), sem("vkh_done"), sem("vkl_done")
        out_done, att_done = sem("out_done"), sem("att_done")
        t_done, th_done, tl_done = sem("t_done"), sem("th_done"), sem("tl_done")
        tc_done, tp_done = sem("tc_done"), sem("tp_done")
        wph_done, wpl_done = sem("wph_done"), sem("wpl_done")
        proj_done, h2_done, mv2_done, sd2_done, rs2_done, x2_done = (
            sem("proj_done"), sem("h2_done"), sem("mv2_done"), sem("sd2_done"), sem("rs2_done"), sem("x2_done"))
        upsgn_done, dnsgn_done, up_done, dn_done = sem("upsgn_done"), sem("dnsgn_done"), sem("up_done"), sem("dn_done")
        relu_done, hidh_done, hidl_done, acc_done, mul_done, fin_done = (
            sem("relu_done"), sem("hidh_done"), sem("hidl_done"), sem("acc_done"), sem("mul_done"), sem("fin_done"))
        fin_v = sem("fin_v")
        v_step = sem("v_step")

        order = [("kq", u) for u in range(4)] + [("M", 1), ("M", 2), ("kq", 4), ("kq", 5), ("G", 0), ("kq", 6), ("kq", 7),
                                                 ("G", 1), ("kq", 8), ("kq", 9), ("VK", 0), ("kq", 10), ("kq", 11), ("VK", 1)]
        order += [("kq", 12), ("out", 0), ("kq", 13), ("G", 2), ("out", 1), ("aT", 0), ("kq", 14),
                  ("kq", 15), ("G", 3), ("aT", 1), ("out", 2), ("VK", 2), ("out", 3), ("aT", 2), ("proj", 0),
                  ("ln", 0), ("proj", 1)]
        pe_order = order + [("aT", 3), ("proj", 2), ("xT", 0), ("out", 4), ("xT", 1), ("proj", 3), ("xT", 2),
                            ("VK", 3), ("out", 5), ("early up", 0), ("xT", 3), ("early up", 1), ("aT", 4)]
        order += [("ln", 1), ("aT", 3), ("xT", 0), ("proj", 2), ("ln", 2), ("xT", 1), ("proj", 3), ("xT", 2), ("VK", 3),
                  ("ln", 3), ("out", 4), ("xT", 3), ("out", 5), ("aT", 4)]
        shared = [key for key in order if key[0] in ("G", "aT", "xT")]
        side = [[]]
        for i in range(TPC, TT):
            side += [[("proj", i)], [("out", i + 1)] * (TPC < i < TT - 1) + [("ln", i)], [], [("aT", i + 1)] * (i + 1 < TT),
                     [("xT", i)]]
        ffn = [("up", 0), ("up", 1)] + [(kind, s + (kind == "up") * 2) for s in range(10) for kind in ("down", "up")]
        for step, more in zip(ffn, side + [[]]):
            order += [step] + more
            pe_order += [step] + more
        turns = {key: n for n, key in enumerate([key for key in order if key[0] in ("aT", "xT")])}
        by_pool = [("aT", 2), ("aT", 3)] + [("xT", i) for i in (0, 1, 2, 4, 5, 6)]
        by_vector = [key for key in turns if key not in by_pool]
        kq_bank = 3 * [0, 1, 2, 3] + [2, 3, 0, 1]

        def bank_of(kind, i):
            if (kind, i) in shared:
                return 4 + shared.index((kind, i)) % 2
            return 6 if kind == "aT" else 7

        def bank_read(key):
            if key[0] == "G":
                return gl_done, key[1] + 1
            return (tc_done, by_pool.index(key) + 1) if key in by_pool else low_half(key)

        def low_half(key):
            return (tp_done, by_pool.index(key) + 1) if key in by_pool else (tl_done, by_vector.index(key) + 1)

        acc_bank = [[2, 3, 4, 5], [6, 7, 2, 3]]
        g_cols = [slice(g * P, (g + 1) * P) for g in range(CT)]
        x2t = [(x2t0_hi, x2t0_lo), (x2t1_hi, x2t1_lo)]
        three = [(0, 0), (0, 1), (1, 0)]
        qs, vs, gs, vks, wps, ats, xas, ks = (((q0_hi, q0_lo), (q1_hi, q1_lo)), (v_hi, v_lo), (g_hi, g_lo),
                                              (vk_hi, vk_lo), (wp_hi, wp_lo), (at_hi, at_lo), (xa_hi, xa_lo),
                                              (k_hi, k_lo))

        def is_k(u):
            return u < 4 or 8 <= u < 12

        def k_tile(u):
            return u if u < 4 else u - 4

        def out_banks(i):
            return 2 if i == TPC else 2 * (i % 2) if i < TPC else 6

        def vk_banks(i):
            return 6 if i < B - 1 else 0

        def proj_bank(i):
            return 6 + i % 2 if i < TPC else 7

        def two_banks(first):
            return ps[:, first:first + 2, 0:2 * G1].rearrange("p a (g c) -> p a g c", g=2)

        def transposed(kind, i, part):
            if kind == "aT":
                return ats[part][:, i % 2]
            return x2t[i // TPC][part][:, :, (i % TPC) * P:(i % TPC + 1) * P]

        last_hi, last_lo = (half[:, 0].rearrange("p g c -> p (g c)") for half in ats)
        last_sgn = up_sgn[:, 0].rearrange("p t c -> p (t c)")

        def sums_of(t):
            return scaled[:, t % 2, :] if t < TPC + 2 else att[:, t % 2, :]

        block = ctx.enter_context(nc.Block())

        @block.sync
        def _(sp):
            w_v = w_qkv.rearrange("(t p) c -> p t c", p=P)
            sp.dma_start(blk[:], blocks.rearrange("(t p) j -> p t j", p=P)).then_inc(ld_blk, 16)
            sp.dma_start(bt[PIX:P, :], blocks_t).then_inc(ld_sq, 16)
            sp.dma_start(bt[0:PIX, :], blocks_t).then_inc(ld_bt, 16)
            for i, col in enumerate((C, 0, 2 * C)):
                for half in range(2):
                    rows = slice(2 * half, 2 * half + 2)
                    sp.dma_start(w_sb[:, rows, col:col + C], w_v[:, rows, col:col + C]).then_inc(ld_w[2 * i + half], 16)
                    if i == 0 and half == 0:
                        sp.dma_start(uf_raw[0:PIX, :], uf_t).then_inc(ld_uf, 16)
                        sp.dma_start(uf_raw[PIX:P, :], uf_t).then_inc(ld_uf, 16)
                if i == 0:
                    sp.dma_start(uft[:], uf_tok).then_inc(ld_uft, 16)
            sp.dma_start(bp_b[:], b_proj.to_broadcast([P, C])).then_inc(ld_bp, 16)
            sp.dma_start(wp_raw[:], w_proj.rearrange("(t p) c -> p t c", p=P)).then_inc(ld_wp, 16)
            sp.dma_start(os_b[:], out_scale.to_broadcast([P, 1])).then_inc(ld_os, 16)
            sp.dma_start(us[:], up_scale).then_inc(ld_os, 16)
            sp.wait_ge(m_done, 3)
            sp.wait_ge(u1_lo, 1)
            sp.wait_ge(u2_hi, 1)
            up_v = w_up.rearrange("(t p) c -> p t c", p=P)
            for i in range(4):
                cols = slice(i * HID // 4, (i + 1) * HID // 4)
                sp.dma_start(up_raw[:, :, cols], up_v[:, :, cols]).then_inc(ld_up[i], 16)
            sp.wait_ge(vk_done, B)
            sp.wait_ge(kq_plo, 8)
            dn_v = w_down.rearrange("(t p) c -> p t c", p=P)
            for i, rows in enumerate((slice(0, 2), slice(2, 6), slice(6, 10), slice(10, 16))):
                sp.dma_start(dn_raw[:, rows, :], dn_v[:, rows, :]).then_inc(ld_dn[i], 16)
            sp.wait_ge(h_bias, TT)
            sp.dma_start(ds_b[:], down_scale.to_broadcast([P, C])).then_inc(ld_ds, 16)
            out_v = out.rearrange("(t p) c -> p t c", p=P)
            for t in range(TPC):
                sp.wait_ge(fin_done, t + 1)
                sp.dma_start(out_v[:, t, :], h_sb[:, t, :]).then_inc(st_out, 16)
            for t, finished, count in ((4, fin_done, 5), (6, fin_v, 1), (5, fin_done, 6), (7, fin_v, 2)):
                sp.wait_ge(finished, count)
                sp.dma_start(out_v[:, t, :], h_sb[:, t, :]).then_inc(st_out, 16)
            sp.wait_ge(st_out, 16 * TT)

        @block.gpsimd
        def _(pool):
            nc.gpsimd.memset(shift[:, 0:1], -HALF / K8).then_inc(shift_set, 1)
            pool.wait_ge(shift_set, 1)
            nc.gpsimd.memset(shift[:, 1:2], -HALF).then_inc(shift_set, 1)
            pool.wait_ge(shift_set, 2)
            nc.gpsimd.memset(mean_w[:], 1.0 / C).then_inc(meanw_set, 1)
            pool.wait_ge(meanw_set, 1)
            nc.gpsimd.memset(ba[:], 0.0).then_inc(ba_zero, 1)
            pool.wait_ge(ba_zero, 1)
            nc.gpsimd.memset(pick[:], 0.0).then_inc(pick_0, 1)
            pool.wait_ge(pick_0, 1)
            nc.gpsimd.affine_select(out=pick[0:PIX, :], in_=pick[0:PIX, :], compare_op=ALU.not_equal, fill=-2.0 / PIX,
                                    base=0, pattern=[[-1, P]], channel_multiplier=1).then_inc(pick_1, 1)
            pool.wait_ge(pick_1, 1)
            nc.gpsimd.memset(pick[PIX:P, BIAS:BIAS + 1], 1.0 / PIX).then_inc(pick_set, 1)
            pool.wait_ge(pick_set, 1)
            nc.gpsimd.memset(pick[PIX:P, ONE:ONE + 1], 1.0 / PIX).then_inc(pick_set, 1)
            pool.wait_ge(pick_set, 2)
            nc.gpsimd.memset(hb[ONE:P, :].bitcast(f32), 0.0).then_inc(hb_zero, 1)
            pool.wait_ge(hb_zero, 1)
            nc.gpsimd.memset(mb[ONE:P, :].bitcast(f32), 0.0).then_inc(mb_zero, 1)
            pool.wait_ge(mb_zero, 1)
            pool.wait_ge(ld_uf, 32)
            nc.gpsimd.tensor_scalar(u2[0:PIX, :], uf_raw[0:PIX, :], 1.0, -HALF, ALU.mult, ALU.add).then_inc(u2_hi, 1)
            pool.wait_ge(u2_hi, 1)
            pool.wait_ge(ld_uft, 16)
            nc.gpsimd.tensor_scalar(uft[:], uft[:], 1.0, -HALF, ALU.mult, ALU.add).then_inc(uft_mid, 1)
            pool.wait_ge(uft_mid, 1)
            nc.gpsimd.memset(xa[:], 0.0).then_inc(xa_zero, 1)
            pool.wait_ge(xa_zero, 1)
            nc.gpsimd.memset(v_hi[:].bitcast(f32), 0.0).then_inc(v_zero, 1)
            pool.wait_ge(v_zero, 1)
            nc.gpsimd.memset(v_lo[:].bitcast(f32), 0.0).then_inc(v_zero, 1)
            pool.wait_ge(v_zero, 2)
            nc.gpsimd.memset(v_hi[ONE:ONE + 1, :, P:G1].bitcast(f32), 1.0).then_inc(v_one, 1)
            pool.wait_ge(v_one, 1)
            nc.gpsimd.memset(eps[:], LN_EPS).then_inc(eps_set, 1)
            pool.wait_ge(eps_set, 1)
            nc.gpsimd.memset(ident[:], 0.0).then_inc(ident_0, 1)
            pool.wait_ge(ident_0, 1)
            nc.gpsimd.affine_select(out=ident[:], in_=ident[:], compare_op=ALU.not_equal, fill=1.0, base=0,
                                    pattern=[[-1, P]], channel_multiplier=1).then_inc(ident_set, 1)
            pool.wait_ge(ident_set, 1)
            nc.gpsimd.memset(mask[:], 0.0).then_inc(mask_0, 1)
            pool.wait_ge(mask_0, 1)
            for h in range(NH):
                rows = slice(h * HD, (h + 1) * HD)
                nc.gpsimd.memset(mask[rows, rows], 1.0).then_inc(mask_set, 1)
                pool.wait_ge(mask_set, 2 * h + 1)
                nc.gpsimd.memset(mask[rows, P + h:P + h + 1], 1.0).then_inc(mask_set, 1)
                pool.wait_ge(mask_set, 2 * h + 2)
            pool.wait_ge(ld_wp, 16)
            nc.gpsimd.tensor_scalar(wp_hi[:], wp_raw[:], 1.0, 0.0, ALU.mult, ALU.add).then_inc(wph_done, 1)
            pool.wait_ge(wph_done, 1)
            nc.gpsimd.tensor_tensor(wp_lo[:], wp_raw[:], wp_hi[:].bitcast(f32), ALU.subtract).then_inc(wpl_done, 1)
            pool.wait_ge(ld_bp, 16)

            def add_bias(tiles):
                for t in tiles:
                    pool.wait_ge(h_stat, t + 1)
                    nc.gpsimd.tensor_tensor(h_sb[:, t, :], h_sb[:, t, :], bp_b[:], ALU.add).then_inc(h_bias, 1)

            add_bias(range(TPC))
            for kind, i in order:
                if kind == "kq" and i >= 8:
                    pool.wait_ge(kq_copy, i - 7)
                    if is_k(i):
                        dst, hi = k_lo[:, k_tile(i) % 4, :], k_hi[:, k_tile(i) % 4, :]
                    else:
                        dst, hi = q1_lo[:, i % 4, :], q1_hi[:, i % 4, :]
                    nc.gpsimd.tensor_tensor(dst, kq_full[:, i % 2, :], hi.bitcast(f32), ALU.subtract).then_inc(kq_plo, 1)
                if kind == "VK" and i >= 2:
                    pool.wait_ge(vkh_done, i + 1)
                    pool.wait_ge(out_done, TPB * (i - 1))
                    nc.gpsimd.tensor_tensor(vk_lo[:, i % 2], vk[:], vk_hi[:, i % 2].bitcast(f32),
                                            ALU.subtract).then_inc(vkl_done, 1)
                if (kind, i) in by_pool:
                    n = by_pool.index((kind, i))
                    pool.wait_ge(tc_done, n + 1)
                    nc.gpsimd.tensor_tensor(transposed(kind, i, 1), t_copy[:, n % 2, :].rearrange("p (g c) -> p g c", g=CT),
                                            transposed(kind, i, 0).bitcast(f32), ALU.subtract).then_inc(tp_done, 1)
                if (kind, i) == ("xT", 2):
                    add_bias(range(TPC, TT))
            pool.wait_ge(ld_ds, 16)
            pool.wait_ge(ld_os, 32)
            nc.gpsimd.tensor_scalar(ds_b[:], ds_b[:], os_b[:, 0:1], 0.0, ALU.mult, ALU.add).then_inc(ds_done, 1)
            for t in range(TPC + 2):
                pool.wait_ge(mul_done, t + 1)
                nc.gpsimd.tensor_tensor(h_sb[:, t, :], sums_of(t), h_sb[:, t, :], ALU.add).then_inc(fin_done, 1)

        @block.scalar
        def _(act):
            act.wait_ge(meanw_set, 1)
            nc.scalar.activation(sd0[:], mean_w[:, 0:1], ACT.Sqrt)
            act.wait_ge(ld_blk, 16)
            act.wait_ge(shift_set, 2)
            nc.scalar.activation(sq_junk[:, 0:CT, :], blk[:], ACT.Square, bias=shift[:, 0:1],
                                 scale=1.0 / K8).then_inc(sqb_done, 1)
            act.wait_ge(ba_zero, 1)
            nc.scalar.activation(ba[:, :, 0:PIX], blk[:], ACT.Copy, bias=2.0 * HALF / PIX,
                                 scale=-2.0 / PIX).then_inc(ba_done, 1)
            act.wait_ge(ld_sq, 16)
            nc.scalar.activation(bt[PIX:P, :], bt[PIX:P, :], ACT.Square,
                                 bias=shift[PIX:P, 1:2]).then_inc(bt_done, 1)

            def high_halves(a, b, cols, bank, done, count, hi, lo, dup):
                high_half(a, cols, bank, done, count, hi)
                duplicates(a, b, cols, bank, count, lo, dup)

            def high_half(a, cols, bank, done, count, hi):
                act.wait_ge(done, count)
                nc.scalar.activation(a[0:ONE + 1, cols], ps[0:ONE + 1, bank, :], ACT.Copy).then_inc(hi, 1)

            def duplicates(a, b, cols, bank, count, lo, dup):
                act.wait_ge(lo, count)
                nc.scalar.activation(b[BIAS:BIAS + 1, cols], ps[BIAS:BIAS + 1, bank, :], ACT.Copy).then_inc(dup, 1)
                nc.scalar.activation(a[PIX:P, cols], ps[0:PIX, bank, :], ACT.Copy).then_inc(dup, 1)

            high_halves(ha, hb, slice(0, C), 3, hp_done, 1, hp_hi, hp_lo, hp_dup)
            high_half(ma, slice(0, C), 4, m_done, 1, m_hi)
            act.wait_ge(sqa_done, 1)
            for t in range(TT):
                act.wait_ge(h_done, t + 1)
                nc.scalar.activation(h_sb[:, t, :], ps[:, t % 3, :], ACT.Identity,
                                     bias=sqa[:, t:t + 1]).then_inc(h_out, 1)
            duplicates(ma, mb, slice(0, C), 4, 1, m_lo, m_dup)
            act.wait_ge(ve1_done, 1)
            nc.scalar.activation(sd1[:], ve1[:], ACT.Sqrt).then_inc(sd1_done, 1)
            high_half(ma, slice(C, 2 * C), 5, m_done, 2, m_hi)

            def sign_up(step, c):
                nc.scalar.activation(up_sgn[:, step % 2], up_raw[:, :, bass.ds(c * P, P)], ACT.Sign).then_inc(upsgn_done, 1)

            def sign_down(step, c):
                nc.scalar.activation(dn_sgn[:, step % 2], dn_raw[:, c, :], ACT.Sign).then_inc(dnsgn_done, 1)

            def relu(step, c, wait):
                act.wait_ge(up_done, wait)
                nc.scalar.activation(hid[:, step % 2, :], ps[:, step % 2, :], ACT.Relu,
                                     scale=us[:, bass.ds(c, 1)]).then_inc(relu_done, 1)

            for kind, i in order:
                if kind == "M" and i == 1:
                    duplicates(ma, mb, slice(C, 2 * C), 5, 2, m_lo, m_dup)
                elif kind == "M":
                    act.wait_ge(m_done, 3)
                    act.wait_ge(v_zero, 2)
                    nc.scalar.activation(v_hi[0:BIAS + 1, :, 0:P],
                                         ps[0:BIAS + 1, 6, :].rearrange("p (g c) -> p g c", g=CT),
                                         ACT.Copy).then_inc(vh_done, 1)
                elif kind == "kq":
                    act.wait_ge(kq_done, i + 1)
                    if is_k(i):
                        t = k_tile(i)
                        if t >= 4:
                            act.wait_ge(g_done, (t - 4) // TPB + 1)
                        dst = k_hi[:, t % 4, :]
                    else:
                        dst = qs[i // 8][0][:, i % 4, :]
                    nc.scalar.activation(dst, ps[:, kq_bank[i], :], ACT.Relu).then_inc(kq_hi, 1)
                    if i >= 8:
                        if i == 8:
                            act.wait_ge(xa_done, 1)
                        if i >= 10:
                            act.wait_ge(kq_plo, i - 9)
                        nc.scalar.activation(kq_full[:, i % 2, :], ps[:, kq_bank[i], :], ACT.Relu).then_inc(kq_copy, 1)
                elif kind == "G":
                    act.wait_ge(g_done, i + 1)
                    if i >= 2:
                        act.wait_ge(vk_done, i - 1)
                    nc.scalar.activation(g_hi[0:XW, i % 2, :], ps[0:XW, bank_of("G", i), :],
                                         ACT.Copy).then_inc(gh_done, 1)
                elif kind == "VK":
                    act.wait_ge(vk_full, i + 1)
                    if i >= 2:
                        act.wait_ge(out_done, TPB * (i - 1))
                    nc.scalar.activation(vk_hi[:, i % 2], vk[:], ACT.Copy).then_inc(vkh_done, 1)
                elif kind in ("aT", "xT"):
                    n = turns[(kind, i)]
                    act.wait_ge(t_done, n + 1)
                    src = ps[:, bank_of(kind, i), :].rearrange("p (g c) -> p g c", g=CT)
                    if kind == "aT" and i >= 2:
                        act.wait_ge(proj_done, i - 1)
                    nc.scalar.activation(transposed(kind, i, 0), src, ACT.Copy).then_inc(th_done, 1)
                    if (kind, i) in by_pool:
                        n = by_pool.index((kind, i))
                        if n >= 2:
                            act.wait_ge(tp_done, n - 1)
                        nc.scalar.activation(t_copy[:, n % 2, :], ps[:, bank_of(kind, i), :], ACT.Copy).then_inc(tc_done, 1)
                    if (kind, i) == ("aT", 3):
                        act.wait_ge(kq_done, 16)
                        act.wait_ge(g_done, B)
                        act.wait_ge(ld_up[0], 16)
                        sign_up(0, 0)
                        sign_up(1, 1)
                        act.wait_ge(ld_os, 32)
                    if (kind, i) == ("aT", TPC):
                        act.wait_ge(ld_dn[0], 16)
                        sign_down(0, 0)
                elif kind == "proj":
                    act.wait_ge(mv2_done, i + 1)
                    act.wait_ge(eps_set, 1)
                    nc.scalar.activation(sd2[:, i:i + 1], mv2[:, i, 1:2], ACT.Sqrt, bias=eps[:]).then_inc(sd2_done, 1)
                elif kind == "up":
                    relu(i, i, i + 1)
                    if (i + 2) % 4 == 0:
                        act.wait_ge(ld_up[(i + 2) // 4], 16)
                    sign_up(i + 2, i + 2)
                elif kind == "down":
                    if i >= 1:
                        act.wait_ge(dn_done, i)
                    if i + 1 in (2, 6, 10):
                        act.wait_ge(ld_dn[(i + 1 + 2) // 4], 16)
                    sign_down(i + 1, i + 1)
            for first, downs, pairs in ((0, 0, 5), (ST, ST - 1, 1)):
                with act.Fori(pairs, ST // 2 - 2) as pair:
                    for d in range(2):
                        s = 2 * pair + d
                        act.wait_ge(dn_done, s + downs)
                        sign_down(d + 1, s + 1)
                        relu(d, s + 2, s + (first + 3))
                        sign_up(d, s + 4)
                for d in range(2):
                    s = ST - 4 + d
                    act.wait_ge(dn_done, downs + s)
                    sign_down(d + 1, s + 1)
                    if first and d == 1:
                        act.wait_ge(hidl_done, first + s + 1)
                    relu(d, s + 2, first + s + 3)
                    if first == 0:
                        sign_up(d, d)
                if first == 0:
                    for s in range(4):
                        down = ST - 2 + s
                        if s == 2:
                            act.wait_ge(acc_done, TPC)
                        else:
                            act.wait_ge(dn_done, down - (s == 3))
                        sign_down(down + 1, (down + 1) % ST)
                        relu(s, s, ST + s + 1)
                        sign_up(s, s + 2)
                else:
                    nc.scalar.activation(last_sgn, dn_raw[:, ST - 1, :], ACT.Sign).then_inc(dnsgn_done, 1)

        @block.vector
        def _(dve):
            steps = [0]

            def chain(ins):
                steps[0] += 1
                ins.then_inc(v_step, 1)
                dve.wait_ge(v_step, steps[0])

            def rsqrt(y, t, ve, sd, rs):
                chain(nc.vector.reciprocal(y, sd))
                chain(nc.vector.tensor_tensor(t, y, y, ALU.mult))
                chain(nc.vector.tensor_tensor(t, t, ve, ALU.mult))
                chain(nc.vector.tensor_scalar(t, t, -0.5, 1.5, ALU.mult, ALU.add))
                return nc.vector.tensor_tensor(rs, y, t, ALU.mult)

            nc.vector.memset(u2[PIX:P, :].bitcast(f32), 0.0).then_inc(u2_zero, 1)
            dve.wait_ge(u2_zero, 1)
            nc.vector.memset(u2[BIAS:BIAS + 1, :].bitcast(f32), 1.0).then_inc(u2_set, 1)
            dve.wait_ge(sqb_done, 1)
            dve.wait_ge(ba_zero, 1)
            for col in (BIAS, ONE):
                nc.vector.reduce_sum(ba[:, :, col], sq_junk[:, 0:CT, :], mybir.AxisListType.X).then_inc(ba_sq, 1)
            nc.vector.memset(u2[ONE:ONE + 1, :].bitcast(f32), 1.0).then_inc(u2_set, 1)
            dve.wait_ge(ld_bt, 16)
            nc.vector.tensor_scalar(bt[0:PIX, :], bt[0:PIX, :], -HALF, None, ALU.add).then_inc(bt_mid, 1)
            dve.wait_ge(mean_done, 1)
            nc.vector.tensor_tensor(bc[:], ba[:], ps[:, 7, 0:P].unsqueeze(1).to_broadcast([P, CT, P]),
                                    ALU.subtract).then_inc(bc_done, 1)
            dve.wait_ge(ld_uf, 32)
            nc.vector.tensor_scalar(u1[:], uf_raw[:], -HALF, None, ALU.add).then_inc(u1_hi, 1)
            dve.wait_ge(hp_hi, 1)
            dve.wait_ge(hb_zero, 1)
            nc.vector.tensor_tensor(hb[0:ONE + 1, :], ps[0:ONE + 1, 3, :], ha[0:ONE + 1, :].bitcast(f32),
                                    ALU.subtract).then_inc(hp_lo, 1)
            dve.wait_ge(u1_hi, 1)
            nc.vector.scalar_tensor_tensor(u1[PIX:P, :], uf_raw[PIX:P, :], -HALF, u1[PIX:P, :].bitcast(f32),
                                           op0=ALU.add, op1=ALU.subtract).then_inc(u1_lo, 1)
            dve.wait_ge(uft_mid, 1)
            chain(nc.vector.scalar_tensor_tensor(sq_junk[:], uft[:], 1.0 / PIX, uft[:], op0=ALU.mult, op1=ALU.mult))
            nc.vector.reduce_sum(sqa[:], sq_junk[:], mybir.AxisListType.X).then_inc(sqa_done, 1)

            def m_low(i):
                dve.wait_ge(m_hi, i + 1)
                dve.wait_ge(mb_zero, 1)
                cols = slice(i * C, (i + 1) * C)
                nc.vector.tensor_tensor(mb[0:ONE + 1, cols], ps[0:ONE + 1, 4 + i, :], ma[0:ONE + 1, cols].bitcast(f32),
                                        ALU.subtract).then_inc(m_lo, 1)

            m_low(0)
            for t in range(TT):
                dve.wait_ge(h_out, t + 1)
                nc.vector.bn_stats(st1[:, t, :], h_sb[:, t, :]).then_inc(h_stat, 1)
            dve.wait_ge(h_stat, TT)
            for t in range(TT):
                last = nc.vector.bn_aggr(mv1[:, t, :], st1[:, t, :])
            chain(last)
            nc.vector.tensor_scalar(ve1[:], mv1[:, :, 1], LN_EPS, None, ALU.add).then_inc(ve1_done, 1)

            def features():
                dve.wait_ge(sd1_done, 1)
                dve.wait_ge(ve1_done, 1)
                chain(rsqrt(y1[:], t1[:], ve1[:], sd1[:], rs1[:]))
                chain(nc.vector.tensor_tensor(rr1[:], rs1[:], rs1[:], ALU.mult))
                dve.wait_ge(xa_zero, 1)
                nc.vector.tensor_tensor(xa[:, :, 0:PIX], uft[:], rr1[:].unsqueeze(2).to_broadcast([P, TT, PIX]),
                                        ALU.mult)
                nc.vector.tensor_copy(xa[:, :, BIAS], rr1[:])
                chain(nc.vector.tensor_copy(xa[:, :, ONE], rs1[:]))
                nc.vector.scalar_tensor_tensor(es1[:], ve1[:], ATT_EPS, rs1[:], op0=ALU.mult, op1=ALU.mult)

            def feature_halves():
                chain(nc.vector.tensor_copy(xa_hi[:], xa[:]))
                nc.vector.tensor_tensor(xa_lo[:], xa[:], xa_hi[:].bitcast(f32), ALU.subtract).then_inc(xa_done, 1)

            def hidden(slot, relu_wait, hi_wait):
                split_hidden(hid_hi[:, slot, :], hid_lo[:, slot, :], slot, relu_wait, hi_wait)

            def split_hidden(hi, lo, slot, relu_wait, hi_wait):
                dve.wait_ge(relu_done, relu_wait)
                nc.vector.tensor_copy(hi, hid[:, slot, :]).then_inc(hidh_done, 1)
                dve.wait_ge(hidh_done, hi_wait)
                nc.vector.tensor_tensor(lo, hid[:, slot, :], hi.bitcast(f32), ALU.subtract).then_inc(hidl_done, 1)

            def scale_sums(chunk, i):
                t = chunk * TPC + i
                dve.wait_ge(acc_done, t + 1)
                if t == 0:
                    dve.wait_ge(ds_done, 1)
                if 2 <= t < TPC + 2:
                    dve.wait_ge(fin_done, t - 1)
                nc.vector.tensor_tensor(sums_of(t), ps[:, acc_bank[chunk][i], :], ds_b[:],
                                        ALU.mult).then_inc(mul_done, 1)

            features()
            m_low(1)
            for kind, i in order:
                if kind == "M" and i == 2:
                    dve.wait_ge(vh_done, 1)
                    nc.vector.tensor_tensor(v_lo[0:BIAS + 1, :, 0:P],
                                            ps[0:BIAS + 1, 6, :].rearrange("p (g c) -> p g c", g=CT),
                                            v_hi[0:BIAS + 1, :, 0:P].bitcast(f32), ALU.subtract).then_inc(vl_done, 1)
                elif kind == "kq" and i < 8:
                    if i == 2:
                        feature_halves()
                    dve.wait_ge(kq_hi, i + 1)
                    if is_k(i):
                        t = k_tile(i)
                        dst, hi = k_lo[:, t % 4, :], k_hi[:, t % 4, :]
                    else:
                        hi, dst = (half[:, i % 4, :] for half in qs[i // 8])
                    nc.vector.scalar_tensor_tensor(dst, ps[:, i % 4, :], 0.0, hi.bitcast(f32), op0=ALU.max,
                                                   op1=ALU.subtract).then_inc(kq_lo, 1)
                elif kind == "G":
                    dve.wait_ge(gh_done, i + 1)
                    nc.vector.tensor_tensor(g_lo[0:XW, i % 2, :], ps[0:XW, bank_of("G", i), :],
                                            g_hi[0:XW, i % 2, :].bitcast(f32), ALU.subtract).then_inc(gl_done, 1)
                elif kind == "VK":
                    dve.wait_ge(vk_done, i + 1)
                    if i == 0:
                        dve.wait_ge(mask_set, 2 * NH)
                    else:
                        dve.wait_ge(vkl_done, i)
                    nc.vector.tensor_tensor(vk[:].rearrange("p (a g) c -> p a g c", a=2), two_banks(vk_banks(i)),
                                            mask[:].unsqueeze(1).unsqueeze(1).to_broadcast([P, 2, 2, G1]),
                                            ALU.mult).then_inc(vk_full, 1)
                    if i < 2:
                        dve.wait_ge(vkh_done, i + 1)
                        nc.vector.tensor_tensor(vk_lo[:, i % 2], vk[:], vk_hi[:, i % 2].bitcast(f32),
                                                ALU.subtract).then_inc(vkl_done, 1)
                elif kind == "out":
                    dve.wait_ge(out_done, i + 1)
                    if i == 0:
                        dve.wait_ge(wpl_done, 1)
                    else:
                        dve.wait_ge(att_done, 2 * i)
                    o = two_banks(out_banks(i))
                    chain(nc.vector.tensor_scalar(den[:, i % 2].rearrange("p (a g) h -> p a g h", a=2), o[:, :, :, P:G1],
                                                  es1[:, i:i + 1], None, ALU.add))
                    chain(nc.vector.reciprocal(rden[:, i % 2], den[:, i % 2]))
                    if i >= 2:
                        dve.wait_ge(t_done, turns[("aT", i - 2)] + 1)
                    for a in range(2):
                        nc.vector.tensor_tensor(
                            att[:, i % 2, a * 2 * P:(a + 1) * 2 * P].rearrange("p (g h d) -> p g h d", g=2, h=NH),
                            o[:, a, :, 0:P].rearrange("p g (h d) -> p g h d", h=NH),
                            rden[:, i % 2, 2 * a:2 * a + 2, :].unsqueeze(3).to_broadcast([P, 2, NH, HD]),
                            ALU.mult).then_inc(att_done, 1)
                elif (kind, i) in by_vector:
                    n = turns[(kind, i)]
                    dve.wait_ge(th_done, n + 1)
                    src = ps[:, bank_of(kind, i), :].rearrange("p (g c) -> p g c", g=CT)
                    nc.vector.tensor_tensor(transposed(kind, i, 1), src, transposed(kind, i, 0).bitcast(f32),
                                            ALU.subtract).then_inc(tl_done, 1)
                elif kind == "proj":
                    dve.wait_ge(proj_done, i + 1)
                    dve.wait_ge(h_bias, i + 1)
                    nc.vector.tensor_tensor(h_sb[:, i, :], ps[:, proj_bank(i), :], h_sb[:, i, :],
                                            ALU.add).then_inc(h2_done, 1)
                    dve.wait_ge(h2_done, i + 1)
                    chain(nc.vector.bn_stats(st2[:, i, :], h_sb[:, i, :]))
                    nc.vector.bn_aggr(mv2[:, i, :], st2[:, i, :]).then_inc(mv2_done, 1)
                elif kind == "ln":
                    dve.wait_ge(sd2_done, i + 1)
                    one = slice(i, i + 1)
                    y, t = y2[:, one], t2[:, one]
                    dve.wait_ge(mv2_done, i + 1)
                    chain(nc.vector.reciprocal(y, sd2[:, one]))
                    chain(nc.vector.scalar_tensor_tensor(t, mv2[:, i, 1:2], LN_EPS, y, op0=ALU.add, op1=ALU.mult))
                    chain(nc.vector.scalar_tensor_tensor(t, t, -0.5, y, op0=ALU.mult, op1=ALU.mult))
                    nc.vector.scalar_tensor_tensor(rs2[:, one], t, 1.5, y, op0=ALU.add, op1=ALU.mult).then_inc(rs2_done, 1)
                    dve.wait_ge(rs2_done, i + 1)
                    if i == 0:
                        dve.wait_ge(kq_done, 16)
                    if i >= 2:
                        dve.wait_ge(t_done, turns[("xT", i - 2)] + 1)
                    nc.vector.tensor_scalar(x2[:, i % 2, :], h_sb[:, i, :], mv2[:, i, 0:1], rs2[:, i:i + 1],
                                            ALU.subtract, ALU.mult).then_inc(x2_done, 1)
                elif kind == "up":
                    if i >= 2:
                        dve.wait_ge(dn_done, i - 1)
                    hidden(i % 2, i + 1, i + 1)

            for chunk, downs, pairs in ((0, 0, 5), (1, ST - 1, 1)):
                first = chunk * ST
                with dve.Fori(pairs, ST // 2 - 1 - chunk) as pair:
                    for d in range(2):
                        s = 2 * pair + d
                        dve.wait_ge(dn_done, s + (downs + 1))
                        hidden(d, s + (first + 3), s + (first + 3))
                if chunk == 0:
                    for s in range(4):
                        if s == 1:
                            dve.wait_ge(acc_done, TPC)
                        else:
                            dve.wait_ge(dn_done, ST - 1 if s == 0 else ST + s - 2)
                        hidden(s % 2, ST + s + 1, ST + s + 1)
                        if s < 2:
                            scale_sums(0, 2 * s)
                            scale_sums(0, 2 * s + 1)
                else:
                    dve.wait_ge(dn_done, 2 * ST - 4)
                    hidden(0, 2 * ST - 1, 2 * ST - 1)
                    split_hidden(last_hi, last_lo, 1, 2 * ST, 2 * ST)
                    for i in range(TPC):
                        scale_sums(1, i)
                        if i >= 2:
                            t = TPC + i
                            dve.wait_ge(mul_done, t + 1)
                            nc.vector.tensor_tensor(h_sb[:, t, :], sums_of(t), h_sb[:, t, :],
                                                    ALU.add).then_inc(fin_v, 1)

        @block.tensor
        def _(pe):
            mm = nc.tensor.matmul
            pe.wait_ge(meanw_set, 1)
            for _ in range(WARM):
                mm(ps[:, 3, 0:P], mean_w[:], mean_w[:], start=True, stop=True)
            pe.wait_ge(ba_done, 1)
            pe.wait_ge(ba_sq, 2)
            for t in range(CT):
                last = mm(ps[:, 7, 0:P], mean_w[:], ba[:, t, :], start=(t == 0), stop=(t == CT - 1))
            last.then_inc(mean_done, 1)
            pe.wait_ge(bt_done, 1)
            pe.wait_ge(bt_mid, 1)
            pe.wait_ge(pick_set, 2)
            mm(ps[:, 3, :], pick[:], bt[:], start=True, stop=True).then_inc(hp_done, 1)

            def centred(i, tiles=range(CT)):
                col = (C, 0, 2 * C)[i]
                for t in tiles:
                    if t % 2 == 0:
                        pe.wait_ge(ld_w[2 * i + t // 2], 16)
                    last = mm(ps[:, 4 + i, :], bc[:, t, :], w_sb[:, t, col:col + C], start=(t == 0), stop=(t == CT - 1))
                    if t == CT - 1:
                        last.then_inc(m_done, 1)

            pe.wait_ge(bc_done, 1)
            centred(0)
            pe.wait_ge(hp_dup, 2)
            pe.wait_ge(u1_lo, 1)
            pe.wait_ge(u2_hi, 1)
            pe.wait_ge(u2_set, 2)
            for t in range(TT):
                if t == TT // 2:
                    centred(1, range(1))
                if t >= 3:
                    pe.wait_ge(h_out, t - 2)
                cols = slice(t * P, (t + 1) * P)
                mm(ps[:, t % 3, :], u1[:, cols], ha[:], start=True, stop=False)
                mm(ps[:, t % 3, :], u2[:, cols], hb[:], start=False, stop=True).then_inc(h_done, 1)
            centred(1, range(1, CT))

            def up(step, chunk, wait, tokens=slice(0, CH), more=False):
                pe.wait_ge(upsgn_done, wait)
                for t in range(CT):
                    for part in range(2):
                        last = mm(ps[:, step % 2, tokens], up_sgn[:, step % 2, t, :], x2t[chunk][part][:, t, tokens],
                                  start=(part == 0 and t == 0), stop=(part == 1 and t == CT - 1))
                if not more:
                    last.then_inc(up_done, 1)

            def down(step, chunk, wait, begin=False, end=False):
                pe.wait_ge(dnsgn_done, wait)
                pe.wait_ge(hidl_done, wait)
                for i in range(TPC):
                    if begin and chunk == 1 and i == 2:
                        pe.wait_ge(mul_done, 1)
                    if begin and chunk == 1 and i == 3:
                        pe.wait_ge(mul_done, 2)
                    for part, half in enumerate((hid_hi, hid_lo)):
                        last = mm(ps[:, acc_bank[chunk][i], :], half[:, step % 2, i * P:(i + 1) * P],
                                  dn_sgn[:, step % 2, :], start=(begin and part == 0), stop=(end and part == 1))
                    if end:
                        last.then_inc(acc_done, 1)
                if not end:
                    last.then_inc(dn_done, 1)

            for kind, i in pe_order:
                if kind == "M":
                    if i == 2:
                        centred(2)
                elif kind == "kq":
                    if i < 4:
                        pe.wait_ge(h_out, TT)
                    elif i < 12:
                        pe.wait_ge(kq_lo, i - 3)
                    elif i < 14:
                        pe.wait_ge(kq_copy, i - 9)
                    else:
                        pe.wait_ge(att_done, 2)
                    if i in (0, 4):
                        pe.wait_ge(m_dup, 2 if i == 0 else 4)
                    if is_k(i):
                        t = k_tile(i)
                        cols = slice(t * P, (t + 1) * P)
                        mm(ps[:, kq_bank[i], :], u1[:, cols], ma[:, 0:C], start=True, stop=False)
                        mm(ps[:, kq_bank[i], :], u2[:, cols], mb[:, 0:C], start=False, stop=True).then_inc(kq_done, 1)
                    else:
                        chans = slice(C + (i % 4) * P, C + (i % 4 + 1) * P)
                        chunk = i // 8
                        cols = slice(chunk * CH, (chunk + 1) * CH)
                        mm(ps[:, kq_bank[i], :], ma[:, chans], u1[:, cols], start=True, stop=False)
                        mm(ps[:, kq_bank[i], :], mb[:, chans], u2[:, cols], start=False, stop=True).then_inc(kq_done, 1)
                elif kind == "G":
                    n = shared.index((kind, i))
                    if i == 0:
                        pe.wait_ge(xa_done, 1)
                        pe.wait_ge(m_dup, 4)
                    if n >= 2:
                        pe.wait_ge(*bank_read(shared[n - 2]))
                    pe.wait_ge(kq_lo if i < 2 else kq_plo, (2, 4, 2, 4)[i])
                    for n in range(TPB):
                        t = i * TPB + n
                        for j, (a, b) in enumerate(three):
                            last = mm(ps[0:XW, bank_of("G", i), :], xas[a][:, t, :], ks[b][:, t % 4, :],
                                      start=(n == 0 and j == 0), stop=(n == TPB - 1 and j == 2))
                    last.then_inc(g_done, 1)
                elif kind == "VK":
                    if i == 0:
                        pe.wait_ge(vl_done, 1)
                        pe.wait_ge(v_one, 1)
                        pe.wait_ge(bc_done, 1)
                    else:
                        pe.wait_ge(vk_full, i)
                    if i == B - 1:
                        pe.wait_ge(att_done, 2 * (TPC - 1))
                    pe.wait_ge(gl_done, i + 1)
                    o = two_banks(vk_banks(i))
                    for g in range(CT):
                        for j, (a, b) in enumerate(three):
                            last = mm(o[:, g // 2, g % 2, :], gs[a][0:XW, i % 2, g_cols[g]], vs[b][0:XW, g, :],
                                      start=(j == 0), stop=(j == 2))
                    last.then_inc(vk_done, 1)
                elif kind == "out":
                    b_i = i // TPB
                    pe.wait_ge(vkl_done, b_i + 1)
                    if i == 0:
                        pe.wait_ge(kq_lo, 8)
                    elif i == TPC:
                        pe.wait_ge(kq_plo, 8)
                    if i < 3:
                        pe.wait_ge(kq_copy, (2, 6, 8)[i])
                    elif i <= TPC:
                        pe.wait_ge(att_done, 4 if i == 3 else 2 * TPC)
                    else:
                        pe.wait_ge(h2_done, TPC if i == TPC + 1 else i)
                        if i > TPC + 1:
                            pe.wait_ge(*low_half(("aT", i - 1)))
                    o = two_banks(out_banks(i))
                    for g in range(CT):
                        for j, (a, b) in enumerate(three):
                            last = mm(o[:, g // 2, g % 2, :], qs[i // TPC][a][:, g, (i % TPC) * P:(i % TPC + 1) * P],
                                      vks[b][:, b_i % 2, g, :], start=(j == 0), stop=(j == 2))
                    last.then_inc(out_done, 1)
                elif kind in ("aT", "xT"):
                    if (kind, i) in shared:
                        pe.wait_ge(*bank_read(shared[shared.index((kind, i)) - 2]))
                    elif kind == "aT":
                        pe.wait_ge(att_done, 2 * (TPC + 2))
                        pe.wait_ge(h2_done, i)
                    elif i < TT - 1:
                        pe.wait_ge(att_done, 2 * (i + 2))
                    if kind == "aT":
                        pe.wait_ge(att_done, 2 * (i + 1))
                        pe.wait_ge(ident_set, 1)
                        src = att[:, i % 2, :]
                    else:
                        pe.wait_ge(x2_done, i + 1)
                        src = x2[:, i % 2, :]
                    for g in range(CT):
                        last = nc.tensor.transpose(ps[:, bank_of(kind, i), g_cols[g]], src[:, g_cols[g]], ident[:])
                    last.then_inc(t_done, 1)
                elif kind == "proj":
                    if i < 2:
                        pe.wait_ge(vk_full, B - 1)
                        pe.wait_ge(wpl_done, 1)
                    elif i <= TPC:
                        pe.wait_ge(h2_done, i - 1)
                        if i == TPC:
                            pe.wait_ge(att_done, 2 * (TPC + 2))
                    else:
                        pe.wait_ge(*bank_read(("xT", i - 1)))
                    pe.wait_ge(*low_half(("aT", i)))
                    for g in range(CT):
                        for j, (a, b) in enumerate(three):
                            last = mm(ps[:, proj_bank(i), :], ats[a][:, i % 2, g, :], wps[b][:, g, :],
                                      start=(g == 0 and j == 0), stop=(g == CT - 1 and j == 2))
                    last.then_inc(proj_done, 1)
                elif kind == "up":
                    if i < 2:
                        pe.wait_ge(*low_half(("xT", TPC - 2)))
                        pe.wait_ge(*low_half(("xT", TPC - 1)))
                        up(i, 0, i + 1, slice(CH // 2, CH))
                    else:
                        pe.wait_ge(relu_done, i - 1)
                        up(i, 0, i + 1)
                elif kind == "early up":
                    pe.wait_ge(vk_full, B)
                    pe.wait_ge(*low_half(("xT", 1)))
                    up(i, 0, i + 1, slice(0, CH // 2), more=True)
                elif kind == "down":
                    if i == 0:
                        pe.wait_ge(att_done, 2 * (TPC + 1))
                    down(i, 0, i + 1, begin=(i == 0))
            for chunk, pairs in ((0, 5), (1, 1)):
                first = chunk * ST
                with pe.Fori(pairs, ST // 2 - 1 - chunk) as pair:
                    for d in range(2):
                        s = 2 * pair + d
                        down(d, chunk, s + (first + 1))
                        pe.wait_ge(relu_done, s + (first + 1))
                        up(d, chunk, s + (first + 3))
                if chunk == 0:
                    pe.wait_ge(*low_half(("xT", TT - 2)))
                    pe.wait_ge(*low_half(("xT", TT - 1)))
                    for n in range(4):
                        step = ST - 2 + n
                        down(step, step // ST, step + 1, begin=(step == ST), end=(step == ST - 1))
                        pe.wait_ge(relu_done, ST + n - 1)
                        up(n, 1, ST + n + 1)
                else:
                    down(0, 1, 2 * ST - 3)
                    pe.wait_ge(relu_done, 2 * ST - 3)
                    up(0, 1, 2 * ST - 1)
                    pe.wait_ge(relu_done, 2 * ST - 2)
                    up(1, 1, 2 * ST)
                    down(1, 1, 2 * ST - 2)
                    pe.wait_ge(dnsgn_done, 2 * ST - 1)
                    pe.wait_ge(hidl_done, 2 * ST - 1)
                    for i in range(TPC):
                        for half in (hid_hi, hid_lo):
                            mm(ps[:, acc_bank[1][i], :], half[:, 0, i * P:(i + 1) * P], dn_sgn[:, 0, :],
                               start=False, stop=False)
                        if i == 0:
                            pe.wait_ge(dnsgn_done, 2 * ST)
                            pe.wait_ge(hidl_done, 2 * ST)
                        for part, half in enumerate((last_hi, last_lo)):
                            last = mm(ps[:, acc_bank[1][i], :], half[:, i * P:(i + 1) * P], last_sgn,
                                      start=False, stop=(part == 1))
                        last.then_inc(acc_done, 1)


def kernel(x, L0_tok_blocks, L0_attn_w_qkv, L0_attn_w_proj, L0_attn_b_proj, L0_ffn_up_weight, L0_ffn_down_weight,
           L0_ffn_up_scale, L0_ffn_down_scale, L0_ffn_output_scale):
    import numpy as np
    import concourse.bacc as bacc
    from concourse.bass_utils import run_bass_kernel_spmd

    x = np.asarray(x)
    n = HW // K8
    patches = x.reshape(B, n, K8, n, K8)
    uf_t = patches.transpose(2, 4, 0, 1, 3).reshape(PIX, TOK)
    uf_tok = patches.transpose(0, 1, 3, 2, 4).reshape(TT, P, PIX).transpose(1, 0, 2)
    arrays = {
        "uf_t": uf_t,
        "uf_tok": uf_tok,
        "blocks": np.asarray(L0_tok_blocks),
        "blocks_t": np.asarray(L0_tok_blocks).T,
        "w_qkv": np.asarray(L0_attn_w_qkv).T,
        "w_proj": np.asarray(L0_attn_w_proj).T,
        "b_proj": np.asarray(L0_attn_b_proj).reshape(1, C),
        "w_up": np.asarray(L0_ffn_up_weight).T,
        "w_down": np.asarray(L0_ffn_down_weight).T,
        "up_scale": np.asarray(L0_ffn_up_scale).reshape(ST, P).T,
        "down_scale": np.asarray(L0_ffn_down_scale).reshape(1, C),
        "out_scale": np.asarray(L0_ffn_output_scale).reshape(1, 1),
    }
    arrays = {k: np.ascontiguousarray(v) for k, v in arrays.items()}
    nc = bacc.Bacc("TRN2", target_bir_lowering=False, num_devices=1)
    ins = [nc.dram_tensor(k, v.shape, mybir.dt.float32, kind="ExternalInput").ap() for k, v in arrays.items()]
    out = nc.dram_tensor("out", (TOK, C), mybir.dt.float32, kind="ExternalOutput").ap()
    vit_tower(nc, *ins, out)
    r = run_bass_kernel_spmd(nc, [arrays], core_ids=[0])
    return np.asarray(r.results[0]["out"]).reshape(B, L, C)
```
